# Optimizing a Trainium2 kernel written in Bass

```python
import numpy as np
import jax
import jax.numpy as jnp

def _softmax(x, axis=-1):
    return jax.nn.softmax(x, axis=axis)

def _gelu(x):
    return jax.nn.gelu(x, approximate=True)

def _silu(x):
    return jax.nn.silu(x)

def _sigmoid(x):
    return jax.nn.sigmoid(x)

def _layernorm(x, axis=-1, eps=1e-05):
    m = jnp.mean(x, axis=axis, keepdims=True)
    v = jnp.var(x, axis=axis, keepdims=True)
    return (x - m) / jnp.sqrt(v + eps)

def _scatter_add(tgt, idx, src, axis=0):
    return tgt.at[idx].add(src)

def _segment_sum(src, seg, n):
    return jax.ops.segment_sum(src, seg, n)
kernel_name = 'mk_macaron_d1_jaxref_r4_0268c0'

def setup_inputs(seed: int=0):
    np.random.seed(seed)
    _w = jnp.asarray

    def _L0_attn_setup():
        import jax, jax.numpy as jnp
        import numpy as np
        B, T, C = (32, 256, 256)
        N_LAYER, LAYER_ID, FIRST_SA = (12, 3, 1)
        RWKV_K_CLAMP = 60.0
        RWKV_K_EPS = 1e-16

        def _init_params():
            f1 = 3.0 + (LAYER_ID - FIRST_SA) / (N_LAYER - 1 - FIRST_SA) * (1.2 - 3.0)
            f2 = 0.65 + (LAYER_ID - FIRST_SA) / (N_LAYER - 1 - FIRST_SA) * (0.4 - 0.65)
            h = np.arange(C, dtype=np.float64)
            decay_speed = np.power(f2, h / (C - 1) * 7) * f1
            time_decay = np.log(decay_speed).astype(np.float32)
            time_first = np.full((C,), np.log(0.3), dtype=np.float32)
            tm = np.ones((C,), dtype=np.float32)
            tm[:C // 2] = 0.0
            return (jnp.asarray(time_decay), jnp.asarray(time_first), jnp.asarray(tm))

        def _wkv(decay, first_w, y, eps):
            a = jnp.broadcast_to(decay, y.shape)

            def comb(l, r):
                a1, b1 = l
                a2, b2 = r
                return (a1 * a2, a2 * b1 + b2)
            _, S = jax.lax.associative_scan(comb, (a, y), axis=1)
            S_prev = jnp.pad(S, ((0, 0), (1, 0), (0, 0)))[:, :-1]
            return eps + first_w * y + S_prev
        key = jax.random.key(seed)
        ks = jax.random.split(key, 5)
        x = jax.random.normal(ks[0], (B, T, C), dtype=jnp.float32)
        scale = 0.02
        Wk = jax.random.normal(ks[1], (C, C), dtype=jnp.float32) * scale
        Wv = jax.random.normal(ks[2], (C, C), dtype=jnp.float32) * scale
        Wr = jax.random.normal(ks[3], (C, C), dtype=jnp.float32) * scale
        Wo = jax.random.normal(ks[4], (C, C), dtype=jnp.float32) * scale
        time_decay, time_first, time_mix = _init_params()
        return {'x': x, 'time_decay': time_decay, 'time_first': time_first, 'time_mix': time_mix, 'Wk': Wk, 'Wv': Wv, 'Wr': Wr, 'Wo': Wo}
    _L0_attn_in = _L0_attn_setup()

    def _L0_ffn_setup():
        import jax, jax.numpy as jnp
        import numpy as np
        EPS = 1e-05

        @jax.custom_vjp
        def ste_quantize(w):
            scale = jnp.maximum(jnp.mean(jnp.abs(w)), EPS)
            return jnp.clip(jnp.round(w / scale), -1.0, 1.0)

        def _ste_fwd(w):
            return (ste_quantize(w), None)

        def _ste_bwd(_, g):
            return (g,)
        ste_quantize.defvjp(_ste_fwd, _ste_bwd)
        key = jax.random.key(seed)
        k1, k2 = jax.random.split(key)
        x = jax.random.normal(k1, (8, 2048, 256), dtype=jnp.float32)
        weight = jax.random.normal(k2, (256, 256), dtype=jnp.float32) * 0.02
        return {'x': x, 'weight': weight}
    _L0_ffn_in = _L0_ffn_setup()
    _d = {'L0_attn_x': _L0_attn_in['x'], 'L0_attn_time_decay': _L0_attn_in['time_decay'], 'L0_attn_time_first': _L0_attn_in['time_first'], 'L0_attn_time_mix': _L0_attn_in['time_mix'], 'L0_attn_Wk': _L0_attn_in['Wk'], 'L0_attn_Wv': _L0_attn_in['Wv'], 'L0_attn_Wr': _L0_attn_in['Wr'], 'L0_attn_Wo': _L0_attn_in['Wo'], 'L0_ffn_weight': _L0_ffn_in['weight']}
    _x0 = _d['L0_attn_x']
    _d['L0_attn_x'] = jax.random.normal(jax.random.fold_in(jax.random.key(seed), 1), (8, 512, 256), dtype=_x0.dtype)
    del _x0
    return _d

def reference(L0_attn_x, L0_attn_time_decay, L0_attn_time_first, L0_attn_time_mix, L0_attn_Wk, L0_attn_Wv, L0_attn_Wr, L0_attn_Wo, L0_ffn_weight):

    def _L0_attn_ref(x, time_decay, time_first, time_mix, Wk, Wv, Wr, Wo):
        import jax, jax.numpy as jnp
        import numpy as np
        B, T, C = (32, 256, 256)
        N_LAYER, LAYER_ID, FIRST_SA = (12, 3, 1)
        RWKV_K_CLAMP = 60.0
        RWKV_K_EPS = 1e-16

        def _init_params():
            f1 = 3.0 + (LAYER_ID - FIRST_SA) / (N_LAYER - 1 - FIRST_SA) * (1.2 - 3.0)
            f2 = 0.65 + (LAYER_ID - FIRST_SA) / (N_LAYER - 1 - FIRST_SA) * (0.4 - 0.65)
            h = np.arange(C, dtype=np.float64)
            decay_speed = np.power(f2, h / (C - 1) * 7) * f1
            time_decay = np.log(decay_speed).astype(np.float32)
            time_first = np.full((C,), np.log(0.3), dtype=np.float32)
            tm = np.ones((C,), dtype=np.float32)
            tm[:C // 2] = 0.0
            return (jnp.asarray(time_decay), jnp.asarray(time_first), jnp.asarray(tm))

        def _wkv(decay, first_w, y, eps):
            a = jnp.broadcast_to(decay, y.shape)

            def comb(l, r):
                a1, b1 = l
                a2, b2 = r
                return (a1 * a2, a2 * b1 + b2)
            _, S = jax.lax.associative_scan(comb, (a, y), axis=1)
            S_prev = jnp.pad(S, ((0, 0), (1, 0), (0, 0)))[:, :-1]
            return eps + first_w * y + S_prev
        Bn, Tn, Cn = x.shape
        xs = jnp.pad(x, ((0, 0), (1, 0), (0, 0)))[:, :-1]
        xm = x * time_mix + xs * (1.0 - time_mix)
        k = xm @ Wk.T
        v = xm @ Wv.T
        r = xm @ Wr.T
        k = jnp.exp(jnp.minimum(k, RWKV_K_CLAMP))
        kv = k * v
        decay = jnp.exp(-jnp.exp(time_decay))
        first_w = jnp.exp(time_first)
        wkv = _wkv(decay, first_w, kv, 0.0)
        wk = _wkv(decay, first_w, k, RWKV_K_EPS)
        rwkv = jax.nn.sigmoid(r) * (wkv / wk)
        return rwkv @ Wo.T

    def _L0_ffn_ref(x, weight):
        import jax, jax.numpy as jnp
        import numpy as np
        EPS = 1e-05

        @jax.custom_vjp
        def ste_quantize(w):
            scale = jnp.maximum(jnp.mean(jnp.abs(w)), EPS)
            return jnp.clip(jnp.round(w / scale), -1.0, 1.0)

        def _ste_fwd(w):
            return (ste_quantize(w), None)

        def _ste_bwd(_, g):
            return (g,)
        ste_quantize.defvjp(_ste_fwd, _ste_bwd)
        w_ternary = ste_quantize(weight)
        scale = jnp.maximum(jnp.mean(jnp.abs(weight)), EPS)
        return jnp.einsum('bsi,oi->bso', x, w_ternary * scale)
    x = L0_attn_x
    x = x + 0.5 * _L0_ffn_ref(_layernorm(x, axis=-1), L0_ffn_weight)
    x = x + _L0_attn_ref(_layernorm(x, axis=-1), L0_attn_time_decay, L0_attn_time_first, L0_attn_time_mix, L0_attn_Wk, L0_attn_Wv, L0_attn_Wr, L0_attn_Wo)
    x = x + 0.5 * _L0_ffn_ref(_layernorm(x, axis=-1), L0_ffn_weight)
    return x

_drawn_inputs = setup_inputs


def setup_inputs(seed=0):
    import zlib

    import numpy as np

    out = dict(_drawn_inputs(seed))
    spreads = {'L0_attn_time_first': (-1.2039728164672852, 0.6)}
    factors = {'L0_attn_time_decay': 3.859,
     'L0_attn_time_mix': 3.993,
     'L0_attn_Wk': 8.0,
     'L0_attn_Wr': 8.0}
    for name, (base, spread) in spreads.items():
        noise = np.random.default_rng([zlib.crc32(name.encode()), seed]).standard_normal(out[name].shape)
        drawn = base * np.exp(spread * noise) if base else spread * noise
        out[name] = jnp.asarray(drawn.astype(out[name].dtype))
    for name, factor in factors.items():
        out[name] = (out[name] * factor).astype(out[name].dtype)
    return out
```

```python
from contextlib import ExitStack

import numpy as np
import concourse.bass as bass
from concourse import mybir

P = 128
LN_EPS = 1e-5
QUANT_EPS = 1e-5
WKV_EPS = 1e-16
K_CLAMP = 60.0


def reciprocal_constants():
    m = 1.0 / np.log(2.0) - 1.0
    shift = (np.log2(1.0 + m) - m) / 2.0
    low, high = 2.0 ** -shift, 2.0 ** shift
    line = np.polynomial.Polynomial([-(low + high) / (high - low), 2.0 / (high - low)])
    t4 = 8 * line ** 4 - 8 * line ** 2 + 1
    cubic = (1 - t4 / t4(0.0)).coef[1:]
    roots = np.polynomial.Polynomial(cubic).roots()
    root = float(roots[np.argmin(np.abs(roots.imag))].real)
    pair = roots[np.argmax(roots.imag)]
    gain = float(-cubic[3]) / 2.0
    return {
        "guess_scale": float(-np.log(2.0) / 2.0 ** 23),
        "guess_bias": float((127.0 - shift) * np.log(2.0)),
        "root": root,
        "square_scale": gain ** 0.5,
        "square_bias": float(-pair.real) * gain ** 0.5,
        "rest": float(pair.imag ** 2) * gain,
    }


def macaron(nc, x, time_decay, time_first, time_mix, wk_t, wv_t, wr_t, wo_t, ffn_t, out):
    f32, f16, i32 = mybir.dt.float32, mybir.dt.float16, mybir.dt.int32
    ALU = mybir.AluOpType
    ACT = mybir.ActivationFunctionType

    SEQS, T, C = x.shape
    CH = C // P
    TT = T // P
    RC = reciprocal_constants()
    DVE_CONSTS = 6 + CH + 1

    x_dram = x.rearrange("s (j p) c -> s p j c", p=P)
    out_dram = out.rearrange("s (j p) c -> s p j c", p=P)

    ctx = ExitStack()
    with ctx:
        def sb(name, shape, dt=f32):
            return ctx.enter_context(nc.sbuf_tensor(name, shape, dt))

        def sem(name):
            return ctx.enter_context(nc.semaphore(name))

        ident = sb("ident", [P, P])
        ones = sb("ones", [P, P])
        decay_rows = sb("decay_rows", [P, CH, T])
        decay_in = sb("decay_in", [P, CH])
        decay_exp = sb("decay_exp", [P, CH])
        decay = sb("decay", [P, CH])
        first_in = sb("first_in", [P, CH])
        first_w = sb("first_w", [P, CH])
        mix = sb("mix", [P, CH])
        mix_rest = sb("mix_rest", [P, CH])
        half_power = sb("half_power", [P, TT])
        guess_bias = sb("guess_bias", [P, 1])
        square_bias = sb("square_bias", [P, 1])
        eps_col = sb("eps_col", [P, 1])
        w_k = sb("w_k", [P, CH, C])
        w_v = sb("w_v", [P, CH, C])
        w_r = sb("w_r", [P, CH, C])
        w_o = sb("w_o", [P, CH, C])
        w_f = sb("w_f", [P, CH, C])
        w_above = sb("w_above", [P, CH, C])
        w_below = sb("w_below", [P, CH, C])
        w_abs = sb("w_abs", [P, CH, C])
        ternary = sb("ternary", [P, CH, C], f16)
        abs_sum = sb("abs_sum", [P, 1])
        half_scale = sb("half_scale", [P, 1])
        minus_half_scale = sb("minus_half_scale", [P, 1])

        X0 = sb("X0", [P, 2, TT, C])
        X1 = sb("X1", [P, 2, TT, C])
        X2 = sb("X2", [P, 2, TT, C])
        X3 = sb("X3", [P, 2, TT, C])
        XS = [X0, X1, X2, X3]
        Z = [None] + [sb(f"Z{n}", [P, TT, C]) for n in (1, 2, 3)]
        bn = [None] + [sb(f"bn{n}", [P, TT, 6]) for n in (1, 2, 3)]
        mean_var = [None] + [sb(f"mean_var{n}", [P, TT, 2]) for n in (1, 2, 3)]
        var_eps = [None] + [sb(f"var_eps{n}", [P, TT]) for n in (1, 2, 3)]
        rstd = [None] + [sb(f"rstd{n}", [P, TT]) for n in (1, 2, 3)]
        row_sum = sb("row_sum", [P, TT])
        minus_mean = sb("minus_mean", [P, TT])
        square_sum = sb("square_sum", [P, TT])
        unread = sb("unread", [P, 2, TT, C])
        shift = [None] + [sb(f"shift{n}", [P, TT]) for n in (1, 2, 3)]

        z_high = [None, sb("z_high1", [P, CH, T], f16), None, sb("z_high3", [P, CH, T], f16)]
        z_low = [None, sb("z_low1", [P, CH, T], f16), None, sb("z_low3", [P, CH, T], f16)]
        XM = sb("XM", [P, 2, CH, T])
        EK = sb("EK", [P, 2, CH, T])
        KV = sb("KV", [P, 2, CH, T])
        TH = sb("TH", [P, 2, CH, T])
        FK = sb("FK", [P, 2, CH, T])
        SK = sb("SK", [P, 2, CH, T + 1])
        SV = sb("SV", [P, 2, CH, T + 1])
        WK = sb("WK", [P, 2, CH, T])
        WV = sb("WV", [P, 2, CH, T])
        Y0 = sb("Y0", [P, 2, CH, T])
        SS = sb("SS", [P, 2, CH, T])
        QQ = sb("QQ", [P, 2, CH, T])
        F = sb("F", [P, 2, CH, T])

        banks = [ctx.enter_context(nc.psum_tensor(f"bank{i}", [P, T], f32)) for i in range(8)]
        turned = banks[0:2]
        tokens = banks[2:4]
        ring = banks[4:8]

        x_loaded = [sem(f"x_loaded{i}") for i in range(2)]
        weights_loaded = sem("weights_loaded")
        vectors_loaded = sem("vectors_loaded")
        ffn_loaded = sem("ffn_loaded")
        out_stored = [sem(f"out_stored{i}") for i in range(2)]
        gpsimd_consts = sem("gpsimd_consts")
        dve_consts = sem("dve_consts")
        dve_ones = sem("dve_ones")
        act_vectors = sem("act_vectors")
        act_decay = sem("act_decay")
        abs_summed = sem("abs_summed")
        scale_summed = sem("scale_summed")
        scale_ready = sem("scale_ready")
        ternary_parts = sem("ternary_parts")
        ternary_ready = sem("ternary_ready")
        stats_ready = [None] + [sem(f"stats_ready{n}") for n in (1, 2, 3)]
        mean_ready = [None] + [sem(f"mean_ready{n}") for n in (1, 2, 3)]
        var_ready = [None] + [sem(f"var_ready{n}") for n in (1, 2, 3)]
        rstd_ready = [None] + [sem(f"rstd_ready{n}") for n in (1, 2, 3)]
        shift_ready = [None] + [sem(f"shift_ready{n}") for n in (1, 2, 3)]
        z_ready = [None] + [sem(f"z_ready{n}") for n in (1, 2, 3)]
        turned_ready = [None] + [sem(f"turned_ready{n}") for n in (1, 2, 3)]
        row_sum_ready = sem("row_sum_ready")
        minus_mean_ready = sem("minus_mean_ready")
        square_sum_ready = sem("square_sum_ready")
        high_ready = [None, sem("high_ready1"), None, sem("high_ready3")]
        low_ready = [None, sem("low_ready1"), None, sem("low_ready3")]
        product_ready = [None, sem("ffn1_ready"), sem("wo_ready"), sem("ffn3_ready")]
        x_ready = [None] + [sem(f"x{n}_ready") for n in (1, 2, 3)]
        scaled_ready = sem("scaled_ready")
        mixed_ready = sem("mixed_ready")
        k_ready, v_ready, r_ready = sem("k_ready"), sem("v_ready"), sem("r_ready")
        exp_k_ready = sem("exp_k_ready")
        tanh_ready = sem("tanh_ready")
        kv_ready = sem("kv_ready")
        clamped_ready = sem("clamped_ready")
        k_state_ready = sem("k_state_ready")
        v_state_ready = sem("v_state_ready")
        first_k_ready = sem("first_k_ready")
        wk_ready = sem("wk_ready")
        wv_ready = sem("wv_ready")
        gated_ready = sem("gated_ready")
        guess_ready = sem("guess_ready")
        s_ready = sem("s_ready")
        guessed_ready = sem("guessed_ready")
        square_ready = sem("square_ready")
        linear_ready = sem("linear_ready")
        rwkv_ready = sem("rwkv_ready")

        def run_steps(engine, last_lag, step):
            loop_from = 4
            loop_to = SEQS - (SEQS - loop_from) % 2
            for t in range(loop_from):
                step(t, t % 2, lambda lag: 0 <= t - lag < SEQS)
            with engine.Fori(loop_from, loop_to - 1, 2) as t:
                step(t, 0, lambda lag: True)
                step(t + 1, 1, lambda lag: True)
            for t in range(loop_to, SEQS + last_lag):
                step(t, t % 2, lambda lag: 0 <= t - lag < SEQS)

        def beyond(b, n):
            return not isinstance(b, int) or b >= n

        block = ctx.enter_context(nc.Block())

        @block.sync
        def _(sp):
            def load(b, p):
                if beyond(b, 2):
                    sp.wait_ge(x_ready[1], 2 * (b - 1))
                sp.dma_start(X0[:, p], x_dram[bass.ds(b, 1)].rearrange("s p j c -> p (s j) c")
                             if not isinstance(b, int) else x_dram[b]).then_inc(x_loaded[p], 16)

            def store(b, p):
                sp.wait_ge(x_ready[3], 2 * (b + 1))
                sp.dma_start(out_dram[bass.ds(b, 1)].rearrange("s p j c -> p (s j) c")
                             if not isinstance(b, int) else out_dram[b], X3[:, p]).then_inc(out_stored[p], 16)

            sp.dma_start(w_f[:, :, :], ffn_t.rearrange("(k p) o -> p k o", p=P)).then_inc(ffn_loaded, 16)
            for vec, dram in ((decay_in, time_decay), (first_in, time_first), (mix, time_mix)):
                sp.dma_start(vec[:, :], dram).then_inc(vectors_loaded, 16)
            for w, dram in ((w_k, wk_t), (w_v, wv_t), (w_r, wr_t), (w_o, wo_t)):
                sp.dma_start(w[:, :, :], dram.rearrange("(k p) o -> p k o", p=P)).then_inc(weights_loaded, 16)

            def step(t, u, has):
                if has(0):
                    load(t, u)
                if has(4):
                    store(t - 4, (u + 4) % 2)

            run_steps(sp, 4, step)
            for stored in out_stored:
                sp.wait_ge(stored, 8 * SEQS + 1)

        @block.gpsimd
        def _(pool):
            nc.gpsimd.memset(ident[:, :], 0.0).then_inc(gpsimd_consts, 1)
            nc.gpsimd.memset(half_power[:, :], -0.5).then_inc(gpsimd_consts, 1)
            pool.wait_ge(gpsimd_consts, 2)
            nc.gpsimd.affine_select(out=ident[:, :], in_=ident[:, :], compare_op=ALU.not_equal, fill=1.0,
                                    base=0, pattern=[[-1, P]], channel_multiplier=1).then_inc(gpsimd_consts, 1)

            def inverse_std(n, b, p):
                pool.wait_ge(var_ready[n], b + 1)
                if beyond(b, 1):
                    pool.wait_ge(z_ready[n], TT * b)
                nc.gpsimd.tensor_tensor(rstd[n][:, :], var_eps[n][:, :], half_power[:, :],
                                        ALU.pow).then_inc(rstd_ready[n], 1)

            def denominator(b, p, m):
                pool.wait_ge(first_k_ready, CH * b + m + 1)
                pool.wait_ge(k_state_ready, CH * b + m + 1)
                if beyond(b, 2):
                    pool.wait_ge(guess_ready, CH * (b - 1))
                nc.gpsimd.tensor_tensor(WK[:, p, m], FK[:, p, m], SK[:, p, m, 0:T], ALU.add).then_inc(wk_ready, 1)

            def times_guess(b, p, m):
                pool.wait_ge(guess_ready, CH * b + m + 1)
                if beyond(b, 2):
                    pool.wait_ge(linear_ready, CH * (b - 1))
                    pool.wait_ge(square_ready, CH * (b - 1))
                nc.gpsimd.tensor_tensor(SS[:, p, m], WK[:, p, m], Y0[:, p, m], ALU.mult).then_inc(s_ready, 1)

            def numerator_times_guess(b, p, m):
                pool.wait_ge(gated_ready, CH * b + m + 1)
                pool.wait_ge(guess_ready, CH * b + m + 1)
                nc.gpsimd.tensor_tensor(WV[:, p, m], WV[:, p, m], Y0[:, p, m],
                                        ALU.mult).then_inc(guessed_ready, 1)

            def step(t, u, has):
                if has(3):
                    inverse_std(3, t - 3, (u + 3) % 2)
                if has(2):
                    times_guess(t - 2, (u + 2) % 2, 0)
                if has(1):
                    inverse_std(2, t - 1, (u + 1) % 2)
                if has(2):
                    denominator(t - 2, (u + 2) % 2, 1)
                    times_guess(t - 2, (u + 2) % 2, 1)
                if has(0):
                    inverse_std(1, t, u)
                if has(2):
                    numerator_times_guess(t - 2, (u + 2) % 2, 1)
                if has(1):
                    denominator(t - 1, (u + 1) % 2, 0)
                    numerator_times_guess(t - 1, (u + 1) % 2, 0)

            run_steps(pool, 3, step)

        @block.scalar
        def _(act):
            act.wait_ge(vectors_loaded, 48)
            nc.scalar.activation(decay_exp[:, :], decay_in[:, :], ACT.Exp).then_inc(act_vectors, 1)
            nc.scalar.activation(first_w[:, :], first_in[:, :], ACT.Exp).then_inc(act_vectors, 1)
            act.wait_ge(act_vectors, 2)
            nc.scalar.activation(decay[:, :], decay_exp[:, :], ACT.Exp, scale=-1.0).then_inc(act_decay, 1)
            act.wait_ge(ffn_loaded, 16)
            nc.scalar.activation(w_abs[:, :, :], w_f[:, :, :], ACT.Abs,
                                 accum_out=abs_sum[:, :]).then_inc(abs_summed, 1)

            def normalize(n, b, p):
                act.wait_ge(shift_ready[n], b + 1)
                if beyond(b, 1):
                    act.wait_ge(turned_ready[n], b)
                for j in range(TT):
                    nc.scalar.activation(Z[n][:, j], XS[n - 1][:, p, j], ACT.Identity, bias=shift[n][:, j:j + 1],
                                         scale=rstd[n][:, j:j + 1]).then_inc(z_ready[n], 1)

            def sum_rows(b, p, j):
                act.wait_ge(x_ready[3 - 1], 2 * b + j // 2 + 1)
                if beyond(b, 1):
                    act.wait_ge(minus_mean_ready, b)
                nc.scalar.activation(unread[:, 0, j], XS[3 - 1][:, p, j], ACT.Copy,
                                     accum_out=row_sum[:, j:j + 1]).then_inc(row_sum_ready, 1)

            def sum_squares(b, p, j):
                act.wait_ge(minus_mean_ready, b + 1)
                if beyond(b, 1):
                    act.wait_ge(var_ready[3], b)
                nc.scalar.activation(unread[:, 1, j], XS[3 - 1][:, p, j], ACT.Square, bias=minus_mean[:, j:j + 1],
                                     accum_out=square_sum[:, j:j + 1]).then_inc(square_sum_ready, 1)

            def high_half(n, b, p, m):
                act.wait_ge(turned_ready[n], b + 1)
                if beyond(b, 1):
                    act.wait_ge(product_ready[n], 2 * b)
                nc.scalar.activation(z_high[n][:, m], turned[m][:, :], ACT.Copy).then_inc(high_ready[n], 1)

            def scale_mix(b, p, m):
                act.wait_ge(turned_ready[2], b + 1)
                if beyond(b, 2):
                    act.wait_ge(r_ready, CH * (b - 1))
                nc.scalar.activation(XM[:, p, m], turned[m][:, :], ACT.Identity,
                                     scale=mix[:, m:m + 1]).then_inc(scaled_ready, 1)

            def exp_k(b, p, m):
                act.wait_ge(clamped_ready, CH * b + m + 1)
                nc.scalar.activation(EK[:, p, m], EK[:, p, m], ACT.Exp).then_inc(exp_k_ready, 1)

            def first_k(b, p, m):
                act.wait_ge(exp_k_ready, CH * b + m + 1)
                if beyond(b, 2):
                    act.wait_ge(wk_ready, CH * (b - 1))
                nc.scalar.activation(FK[:, p, m], EK[:, p, m], ACT.Identity, scale=first_w[:, m:m + 1],
                                     bias=eps_col[:, :]).then_inc(first_k_ready, 1)

            def tanh_r(b, p, m):
                act.wait_ge(r_ready, CH * b + m + 1)
                if beyond(b, 2):
                    act.wait_ge(gated_ready, CH * (b - 1))
                nc.scalar.activation(TH[:, p, m], ring[(2 * p + 3 * m + 2) % 4][:, :], ACT.Tanh,
                                     scale=-0.5).then_inc(tanh_ready, 1)

            def guess(b, p, m):
                act.wait_ge(wk_ready, CH * b + m + 1)
                if beyond(b, 2):
                    act.wait_ge(s_ready, CH * (b - 1))
                    act.wait_ge(guessed_ready, CH * (b - 1))
                nc.scalar.activation(Y0[:, p, m], WK[:, p, m].bitcast(i32), ACT.Exp, scale=RC["guess_scale"],
                                     bias=guess_bias[:, :]).then_inc(guess_ready, 1)

            def square(b, p, m):
                act.wait_ge(s_ready, CH * b + m + 1)
                if beyond(b, 2):
                    act.wait_ge(rwkv_ready, CH * (b - 1))
                nc.scalar.activation(QQ[:, p, m], SS[:, p, m], ACT.Square,
                                     scale=RC["square_scale"], bias=square_bias[:, :]).then_inc(square_ready, 1)

            act.wait_ge(dve_consts, DVE_CONSTS)

            def step(t, u, has):
                if has(2):
                    square(t - 2, (u + 2) % 2, 1)
                if has(0):
                    normalize(1, t, u)
                if has(1):
                    exp_k(t - 1, (u + 1) % 2, 0)
                    first_k(t - 1, (u + 1) % 2, 0)
                if has(0):
                    high_half(1, t, u, 0)
                    high_half(1, t, u, 1)
                if has(2):
                    sum_rows(t - 2, (u + 2) % 2, 0)
                if has(1):
                    guess(t - 1, (u + 1) % 2, 0)
                if has(2):
                    sum_rows(t - 2, (u + 2) % 2, 1)
                    sum_rows(t - 2, (u + 2) % 2, 2)
                    sum_rows(t - 2, (u + 2) % 2, 3)
                if has(1):
                    tanh_r(t - 1, (u + 1) % 2, 0)
                if has(2):
                    sum_squares(t - 2, (u + 2) % 2, 0)
                    sum_squares(t - 2, (u + 2) % 2, 1)
                    sum_squares(t - 2, (u + 2) % 2, 2)
                    sum_squares(t - 2, (u + 2) % 2, 3)
                if has(1):
                    exp_k(t - 1, (u + 1) % 2, 1)
                    first_k(t - 1, (u + 1) % 2, 1)
                if has(2):
                    normalize(3, t - 2, (u + 2) % 2)
                    high_half(3, t - 2, (u + 2) % 2, 0)
                    high_half(3, t - 2, (u + 2) % 2, 1)
                if has(0):
                    normalize(2, t, u)
                if has(1):
                    guess(t - 1, (u + 1) % 2, 1)
                    tanh_r(t - 1, (u + 1) % 2, 1)
                if has(0):
                    scale_mix(t, u, 0)
                    scale_mix(t, u, 1)
                if has(1):
                    square(t - 1, (u + 1) % 2, 0)

            run_steps(act, 2, step)

        @block.vector
        def _(dve):
            nc.vector.memset(ones[:, :], 1.0).then_inc(dve_ones, 1)
            nc.vector.memset(guess_bias[:, :], RC["guess_bias"]).then_inc(dve_consts, 1)
            nc.vector.memset(square_bias[:, :], RC["square_bias"]).then_inc(dve_consts, 1)
            nc.vector.memset(eps_col[:, :], WKV_EPS).then_inc(dve_consts, 1)
            nc.vector.memset(decay_rows[:, :, :], 1.0).then_inc(dve_consts, 1)
            for parity, stored in enumerate(out_stored):
                nc.vector.memset(X3[:, parity, 0, 0:1], 0.0).then_inc(stored, 1)
            for state in (SK, SV):
                nc.vector.memset(state[:, :, :, 0:1], 0.0).then_inc(dve_consts, 1)
            dve.wait_ge(act_decay, 1)
            dve.wait_ge(dve_consts, 6)
            for m in range(CH):
                nc.vector.tensor_scalar(decay_rows[:, m], decay_rows[:, m], decay[:, m:m + 1], None,
                                        ALU.mult).then_inc(dve_consts, 1)
            nc.vector.tensor_scalar(mix_rest[:, :], mix[:, :], -1.0, 1.0, ALU.mult, ALU.add).then_inc(dve_consts, 1)
            dve.wait_ge(scale_summed, 1)
            nc.vector.tensor_scalar(half_scale[:, :], tokens[0][:, 0:1], 0.5 / (C * C), 0.5 * QUANT_EPS, ALU.mult,
                                    ALU.max).then_inc(scale_ready, 1)
            dve.wait_ge(scale_ready, 1)
            nc.vector.tensor_scalar(minus_half_scale[:, :], half_scale[:, :], -1.0, None,
                                    ALU.mult).then_inc(scale_ready, 1)
            nc.vector.tensor_scalar(w_above[:, :, :], w_f[:, :, :], half_scale[:, :], None,
                                    ALU.is_gt).then_inc(ternary_parts, 1)
            dve.wait_ge(scale_ready, 2)
            nc.vector.tensor_scalar(w_below[:, :, :], w_f[:, :, :], minus_half_scale[:, :], None,
                                    ALU.is_lt).then_inc(ternary_parts, 1)
            dve.wait_ge(ternary_parts, 2)
            nc.vector.tensor_tensor(ternary[:, :, :], w_above[:, :, :], w_below[:, :, :],
                                    ALU.subtract).then_inc(ternary_ready, 1)

            def stats(n, b, p, j):
                if n == 1:
                    dve.wait_ge(x_loaded[p], 8 * (b - p) + 16)
                else:
                    dve.wait_ge(x_ready[n - 1], 2 * b + j // 2 + 1)
                nc.vector.bn_stats(bn[n][:, j], XS[n - 1][:, p, j]).then_inc(stats_ready[n], 1)

            def variance(n, b, p):
                dve.wait_ge(stats_ready[n], TT * (b + 1))
                dve.nop(nofuse=True)
                for j in range(TT):
                    nc.vector.bn_aggr(mean_var[n][:, j], bn[n][:, j]).then_inc(mean_ready[n], 1)
                dve.wait_ge(mean_ready[n], TT * (b + 1))
                if beyond(b, 1):
                    dve.wait_ge(rstd_ready[n], b)
                nc.vector.tensor_scalar(var_eps[n][:, :], mean_var[n][:, :, 1], LN_EPS, None,
                                        ALU.add).then_inc(var_ready[n], 1)

            def negate_mean(b, p):
                dve.wait_ge(row_sum_ready, TT * (b + 1))
                if beyond(b, 1):
                    dve.wait_ge(square_sum_ready, TT * b)
                nc.vector.tensor_scalar(minus_mean[:, :], row_sum[:, :], -1.0 / C, None,
                                        ALU.mult).then_inc(minus_mean_ready, 1)

            def variance_of_squares(b, p):
                dve.wait_ge(square_sum_ready, TT * (b + 1))
                if beyond(b, 1):
                    dve.wait_ge(rstd_ready[3], b)
                nc.vector.tensor_scalar(var_eps[3][:, :], square_sum[:, :], 1.0 / C, LN_EPS, ALU.mult,
                                        ALU.add).then_inc(var_ready[3], 1)

            def shifts(n, b, p):
                dve.wait_ge(rstd_ready[n], b + 1)
                if beyond(b, 1):
                    dve.wait_ge(z_ready[n], TT * b)
                if n == 3:
                    dve.wait_ge(minus_mean_ready, b + 1)
                    nc.vector.tensor_tensor(shift[n][:, :], minus_mean[:, :], rstd[n][:, :],
                                            ALU.mult).then_inc(shift_ready[n], 1)
                else:
                    nc.vector.scalar_tensor_tensor(shift[n][:, :], mean_var[n][:, :, 0], -1.0, rstd[n][:, :],
                                                   ALU.mult, ALU.mult).then_inc(shift_ready[n], 1)

            def low_half(n, b, p, m):
                dve.wait_ge(high_ready[n], CH * b + m + 1)
                if beyond(b, 1):
                    dve.wait_ge(product_ready[n], 2 * b)
                nc.vector.tensor_tensor(z_low[n][:, m], turned[m][:, :], z_high[n][:, m],
                                        ALU.subtract).then_inc(low_ready[n], 1)

            def residual(n, b, p, h):
                dve.wait_ge(product_ready[n], 2 * b + h + 1)
                if n == 1:
                    dve.wait_ge(z_ready[1], TT * (b + 1))
                if n == 3 and beyond(b, 2):
                    dve.wait_ge(out_stored[p], 8 * (b - p) + 1)
                if n < 3 and beyond(b, 2):
                    dve.wait_ge(z_ready[n + 1], TT * (b - 1))
                    dve.wait_ge(x_ready[n + 1], 2 * (b - 1))
                old = XS[n - 1][:, p, 2 * h:2 * h + 2]
                new = XS[n][:, p, 2 * h:2 * h + 2]
                bank = tokens[h][:, :].rearrange("p (j c) -> p j c", c=C)
                if n == 2:
                    nc.vector.tensor_tensor(new, bank, old, ALU.add).then_inc(x_ready[n], 1)
                else:
                    nc.vector.scalar_tensor_tensor(new, bank, half_scale[:, :], old, ALU.mult,
                                                   ALU.add).then_inc(x_ready[n], 1)

            def token_mix(b, p, m):
                dve.wait_ge(scaled_ready, CH * b + m + 1)
                nc.vector.scalar_tensor_tensor(XM[:, p, m, 1:T], turned[m][:, 0:T - 1], mix_rest[:, m:m + 1],
                                               XM[:, p, m, 1:T], ALU.mult, ALU.add).then_inc(mixed_ready, 1)

            def clamp_k(b, p, m):
                dve.wait_ge(k_ready, CH * b + m + 1)
                if beyond(b, 2):
                    dve.wait_ge(k_state_ready, CH * (b - 1))
                    dve.wait_ge(first_k_ready, CH * (b - 1))
                nc.vector.tensor_scalar(EK[:, p, m], ring[(2 * p + 3 * m) % 4][:, :], K_CLAMP, None,
                                        ALU.min).then_inc(clamped_ready, 1)

            def key_value(b, p, m):
                dve.wait_ge(exp_k_ready, CH * b + m + 1)
                dve.wait_ge(v_ready, CH * b + m + 1)
                nc.vector.tensor_tensor(KV[:, p, m], EK[:, p, m], ring[(2 * p + 3 * m + 1) % 4][:, :],
                                        ALU.mult).then_inc(kv_ready, 1)

            def k_state(b, p, m):
                dve.wait_ge(exp_k_ready, CH * b + m + 1)
                if beyond(b, 2):
                    dve.wait_ge(wk_ready, CH * (b - 1))
                nc.vector.tensor_tensor_scan(SK[:, p, m, 1:T + 1], decay_rows[:, m], EK[:, p, m], 0.0, ALU.mult,
                                             ALU.add).then_inc(k_state_ready, 1)

            def v_state(b, p, m):
                dve.wait_ge(kv_ready, CH * b + m + 1)
                nc.vector.tensor_tensor_scan(SV[:, p, m, 1:T + 1], decay_rows[:, m], KV[:, p, m], 0.0, ALU.mult,
                                             ALU.add).then_inc(v_state_ready, 1)

            def numerator(b, p, m):
                dve.wait_ge(v_state_ready, CH * b + m + 1)
                nc.vector.scalar_tensor_tensor(WV[:, p, m], KV[:, p, m], first_w[:, m:m + 1], SV[:, p, m, 0:T],
                                               ALU.mult, ALU.add).then_inc(wv_ready, 1)

            def gate(b, p, m):
                dve.wait_ge(tanh_ready, CH * b + m + 1)
                dve.wait_ge(wv_ready, CH * b + m + 1)
                nc.vector.scalar_tensor_tensor(WV[:, p, m], TH[:, p, m], -1.0, WV[:, p, m], ALU.add,
                                               ALU.mult).then_inc(gated_ready, 1)

            def linear(b, p, m):
                dve.wait_ge(guessed_ready, CH * b + m + 1)
                dve.wait_ge(s_ready, CH * b + m + 1)
                nc.vector.scalar_tensor_tensor(WV[:, p, m], SS[:, p, m], -RC["root"], WV[:, p, m], ALU.add,
                                               ALU.mult).then_inc(linear_ready, 1)

            def rwkv(b, p, m):
                dve.wait_ge(square_ready, CH * b + m + 1)
                dve.wait_ge(linear_ready, CH * b + m + 1)
                if beyond(b, 2):
                    dve.wait_ge(product_ready[2], 2 * (b - 1))
                nc.vector.scalar_tensor_tensor(F[:, p, m], QQ[:, p, m], RC["rest"], WV[:, p, m], ALU.add,
                                               ALU.mult).then_inc(rwkv_ready, 1)

            def step(t, u, has):
                if has(3):
                    negate_mean(t - 3, (u + 3) % 2)
                if has(0):
                    stats(1, t, u, 0)
                if has(2):
                    gate(t - 2, (u + 2) % 2, 0)
                if has(0):
                    stats(1, t, u, 1)
                if has(2):
                    clamp_k(t - 2, (u + 2) % 2, 1)
                if has(3):
                    variance_of_squares(t - 3, (u + 3) % 2)
                if has(1):
                    residual(1, t - 1, (u + 1) % 2, 0)
                    stats(2, t - 1, (u + 1) % 2, 0)
                if has(3):
                    shifts(3, t - 3, (u + 3) % 2)
                if has(1):
                    residual(1, t - 1, (u + 1) % 2, 1)
                    stats(2, t - 1, (u + 1) % 2, 1)
                    stats(2, t - 1, (u + 1) % 2, 2)
                    stats(2, t - 1, (u + 1) % 2, 3)
                    variance(2, t - 1, (u + 1) % 2)
                if has(2):
                    key_value(t - 2, (u + 2) % 2, 1)
                if has(0):
                    stats(1, t, u, 2)
                if has(2):
                    v_state(t - 2, (u + 2) % 2, 1)
                if has(1):
                    shifts(2, t - 1, (u + 1) % 2)
                if has(2):
                    k_state(t - 2, (u + 2) % 2, 1)
                if has(3):
                    low_half(3, t - 3, (u + 3) % 2, 0)
                    low_half(3, t - 3, (u + 3) % 2, 1)
                if has(0):
                    stats(1, t, u, 3)
                if has(2):
                    numerator(t - 2, (u + 2) % 2, 1)
                    linear(t - 2, (u + 2) % 2, 0)
                if has(0):
                    variance(1, t, u)
                if has(1):
                    token_mix(t - 1, (u + 1) % 2, 0)
                    token_mix(t - 1, (u + 1) % 2, 1)
                if has(2):
                    gate(t - 2, (u + 2) % 2, 1)
                if has(0):
                    shifts(1, t, u)
                if has(2):
                    rwkv(t - 2, (u + 2) % 2, 0)
                if has(3):
                    residual(3, t - 3, (u + 3) % 2, 0)
                if has(1):
                    clamp_k(t - 1, (u + 1) % 2, 0)
                if has(2):
                    linear(t - 2, (u + 2) % 2, 1)
                    rwkv(t - 2, (u + 2) % 2, 1)
                if has(3):
                    residual(3, t - 3, (u + 3) % 2, 1)
                if has(1):
                    k_state(t - 1, (u + 1) % 2, 0)
                    key_value(t - 1, (u + 1) % 2, 0)
                if has(0):
                    low_half(1, t, u, 0)
                if has(2):
                    residual(2, t - 2, (u + 2) % 2, 0)
                if has(1):
                    v_state(t - 1, (u + 1) % 2, 0)
                if has(2):
                    residual(2, t - 2, (u + 2) % 2, 1)
                if has(0):
                    low_half(1, t, u, 1)
                if has(1):
                    numerator(t - 1, (u + 1) % 2, 0)

            run_steps(dve, 3, step)

        @block.tensor
        def _(pe):
            pe.wait_ge(dve_ones, 1)
            pe.wait_ge(abs_summed, 1)
            nc.tensor.matmul(tokens[0][:, 0:1], ones[:, :], abs_sum[:, :], start=True, stop=True).then_inc(scale_summed, 1)
            pe.wait_ge(gpsimd_consts, 3)

            def bank_free(readers, per_batch, b, upto):
                if isinstance(b, int):
                    if b < 0:
                        return
                    b = min(b, SEQS - 1)
                pe.wait_ge(readers, per_batch * b + upto)

            def turn(n, b, p, after):
                for m, last_b in after.items():
                    bank_free(mixed_ready if m == 2 else low_ready[m], CH, last_b, CH)
                for j in range(TT):
                    pe.wait_ge(z_ready[n], TT * b + j + 1)
                    for m in range(CH):
                        last = nc.tensor.transpose(turned[m][:, j * P:(j + 1) * P], Z[n][:, j, m * P:(m + 1) * P],
                                                   ident[:, :])
                last.then_inc(turned_ready[n], 1)

            def ffn(n, b, p, h, after):
                for m, last_b in after.items():
                    bank_free(x_ready[m], 2, last_b, h + 1)
                pe.wait_ge(low_ready[n], CH * (b + 1))
                for j in (2 * h, 2 * h + 1):
                    o = tokens[h][:, (j % 2) * C:(j % 2 + 1) * C]
                    parts = [(part, m) for m in range(CH) for part in (z_high[n], z_low[n])]
                    for i, (part, m) in enumerate(parts):
                        last = nc.tensor.matmul(o, part[:, m, j * P:(j + 1) * P], ternary[:, m],
                                                start=i == 0, stop=i == len(parts) - 1)
                last.then_inc(product_ready[n], 1)

            def output_product(b, p, h, after):
                for m, last_b in after.items():
                    bank_free(x_ready[m], 2, last_b, h + 1)
                pe.wait_ge(rwkv_ready, CH * (b + 1))
                for j in (2 * h, 2 * h + 1):
                    o = tokens[h][:, (j % 2) * C:(j % 2 + 1) * C]
                    for m in range(CH):
                        last = nc.tensor.matmul(o, F[:, p, m, j * P:(j + 1) * P], w_o[:, m],
                                                start=m == 0, stop=m == CH - 1)
                last.then_inc(product_ready[2], 1)

            def project(b, p, w, use, ready, readers, b_before, m_before, m):
                if beyond(b, 1) or b_before is b:
                    pe.wait_ge(readers, CH * b_before + m_before + 1)
                pe.wait_ge(mixed_ready, CH * (b + 1))
                for c in range(CH):
                    last = nc.tensor.matmul(ring[(2 * p + use) % 4][:, :], w[:, c, m * P:(m + 1) * P], XM[:, p, c],
                                            start=c == 0, stop=c == CH - 1)
                last.then_inc(ready, 1)

            def project_k(b, p, m):
                if m == 0:
                    project(b, p, w_k, 0, k_ready, tanh_ready, b - 1, 0, m)
                else:
                    project(b, p, w_k, 3, k_ready, tanh_ready, b - 1, 1, m)

            def project_v(b, p, m):
                if m == 0:
                    project(b, p, w_v, 1, v_ready, clamped_ready, b - 1, 1, m)
                else:
                    project(b, p, w_v, 4, v_ready, clamped_ready, b, 0, m)

            def project_r(b, p, m):
                if m == 0:
                    project(b, p, w_r, 2, r_ready, kv_ready, b - 1, 1, m)
                else:
                    project(b, p, w_r, 5, r_ready, kv_ready, b, 0, m)

            pe.wait_ge(ternary_ready, 1)
            pe.wait_ge(weights_loaded, 64)

            def step(t, u, has):
                if has(0):
                    turn(1, t, u, after={1: t - 1, 2: t - 1, 3: t - 3})
                if has(2):
                    output_product(t - 2, (u + 2) % 2, 0, after={1: t - 1, 2: t - 3, 3: t - 3})
                    output_product(t - 2, (u + 2) % 2, 1, after={1: t - 1, 2: t - 3, 3: t - 3})
                if has(1):
                    project_r(t - 1, (u + 1) % 2, 0)
                    project_k(t - 1, (u + 1) % 2, 1)
                if has(0):
                    ffn(1, t, u, 0, after={1: t - 1, 2: t - 2, 3: t - 3})
                    ffn(1, t, u, 1, after={1: t - 1, 2: t - 2, 3: t - 3})
                if has(1):
                    project_v(t - 1, (u + 1) % 2, 1)
                if has(2):
                    turn(3, t - 2, (u + 2) % 2, after={1: t, 2: t - 1, 3: t - 3})
                if has(1):
                    project_r(t - 1, (u + 1) % 2, 1)
                if has(0):
                    turn(2, t, u, after={1: t, 2: t - 1, 3: t - 2})
                if has(2):
                    ffn(3, t - 2, (u + 2) % 2, 0, after={1: t, 2: t - 2, 3: t - 3})
                    ffn(3, t - 2, (u + 2) % 2, 1, after={1: t, 2: t - 2, 3: t - 3})
                if has(0):
                    project_k(t, u, 0)
                    project_v(t, u, 0)

            run_steps(pe, 2, step)


_OUT = "out"


def kernel(L0_attn_x, L0_attn_time_decay, L0_attn_time_first, L0_attn_time_mix, L0_attn_Wk, L0_attn_Wv, L0_attn_Wr,
           L0_attn_Wo, L0_ffn_weight):
    import concourse.bacc as bacc
    from concourse.bass_utils import run_bass_kernel_spmd

    def turned(w):
        return np.ascontiguousarray(np.asarray(w).T)

    def by_partition(v):
        return np.ascontiguousarray(np.asarray(v).reshape(-1, P).T)

    arrays = {
        "x": np.ascontiguousarray(L0_attn_x),
        "time_decay": by_partition(L0_attn_time_decay),
        "time_first": by_partition(L0_attn_time_first),
        "time_mix": by_partition(L0_attn_time_mix),
        "wk_t": turned(L0_attn_Wk),
        "wv_t": turned(L0_attn_Wv),
        "wr_t": turned(L0_attn_Wr),
        "wo_t": turned(L0_attn_Wo),
        "ffn_t": turned(L0_ffn_weight),
    }
    nc = bacc.Bacc("TRN2", target_bir_lowering=False, num_devices=1)
    args = [nc.dram_tensor(name, a.shape, mybir.dt.from_np(a.dtype), kind="ExternalInput").ap()
            for name, a in arrays.items()]
    x_shape = arrays["x"].shape
    out = nc.dram_tensor(_OUT, x_shape, mybir.dt.float32, kind="ExternalOutput").ap()
    macaron(nc, *args, out)
    result = run_bass_kernel_spmd(nc, [arrays], core_ids=[0])
    return result.results[0][_OUT]
```

```python
from contextlib import ExitStack

import numpy as np
import concourse.bass as bass
from concourse import mybir

P = 128
LN_EPS = 1e-5
QUANT_EPS = 1e-5
WKV_EPS = 1e-16
K_CLAMP = 60.0
WARM = (8, 16, 12, 14, 18, 9)
NORM_FIRST = (0,)
NORM_LAST = (7,)


def reciprocal_constants():
    m = 1.0 / np.log(2.0) - 1.0
    shift = (np.log2(1.0 + m) - m) / 2.0
    low, high = 2.0 ** -shift, 2.0 ** shift
    line = np.polynomial.Polynomial([-(low + high) / (high - low), 2.0 / (high - low)])
    t4 = 8 * line ** 4 - 8 * line ** 2 + 1
    cubic = (1 - t4 / t4(0.0)).coef[1:]
    roots = np.polynomial.Polynomial(cubic).roots()
    root = float(roots[np.argmin(np.abs(roots.imag))].real)
    pair = roots[np.argmax(roots.imag)]
    gain = float(-cubic[3]) / 2.0
    return {
        "guess_scale": float(-np.log(2.0) / 2.0 ** 23),
        "guess_bias": float((127.0 - shift) * np.log(2.0)),
        "root": root,
        "square_scale": gain ** 0.5,
        "square_bias": float(-pair.real) * gain ** 0.5,
        "rest": float(pair.imag ** 2) * gain,
    }


def macaron(nc, x, time_decay, time_first, time_mix, wk_t, wv_t, wr_t, wo_t, ffn_t, out):
    f32, f16, i32 = mybir.dt.float32, mybir.dt.float16, mybir.dt.int32
    ALU = mybir.AluOpType
    ACT = mybir.ActivationFunctionType

    SEQS, T, C = x.shape
    CH = C // P
    TT = T // P
    RC = reciprocal_constants()
    DVE_CONSTS = 3 + CH + 1

    x_dram = x.rearrange("s (j p) c -> s p j c", p=P)
    out_dram = out.rearrange("s (j p) c -> s p j c", p=P)

    ctx = ExitStack()
    with ctx:
        def sb(name, shape, dt=f32):
            return ctx.enter_context(nc.sbuf_tensor(name, shape, dt))

        def sem(name):
            return ctx.enter_context(nc.semaphore(name))

        ident = sb("ident", [P, P])
        ones = sb("ones", [P, P])
        warm = sb("warm", [P, T], f16)
        decay_rows = sb("decay_rows", [P, CH, T])
        decay_in = sb("decay_in", [P, CH])
        decay_exp = sb("decay_exp", [P, CH])
        decay = sb("decay", [P, CH])
        first_in = sb("first_in", [P, CH])
        first_w = sb("first_w", [P, CH])
        mix = sb("mix", [P, CH])
        mix_rest = sb("mix_rest", [P, CH])
        half_power = sb("half_power", [P, TT])
        w_k = sb("w_k", [P, CH, C])
        w_v = sb("w_v", [P, CH, C])
        w_r = sb("w_r", [P, CH, C])
        w_o = sb("w_o", [P, CH, C])
        w_f = sb("w_f", [P, CH, C])
        w_below = sb("w_below", [P, CH, C])
        w_abs = sb("w_abs", [P, CH, C])
        ternary = sb("ternary", [P, CH, C], f16)
        abs_sum = sb("abs_sum", [P, 1])
        half_scale = sb("half_scale", [P, 1])
        minus_half_scale = sb("minus_half_scale", [P, 1])

        X0 = sb("X0", [P, 2, TT, C])
        X1 = sb("X1", [P, 2, TT, C])
        X2 = sb("X2", [P, 2, TT, C])
        X3 = sb("X3", [P, 2, TT, C])
        X1_held = sb("X1_held", [P, 2, TT, C])
        XS = [X0, X1, X2, X3]
        Z = [None] + [sb(f"Z{n}", [P, TT, C]) for n in (1, 2, 3)]
        bn = [None] + [sb(f"bn{n}", [P, TT, 6]) for n in (1, 2, 3)]
        mean_var = [None] + [sb(f"mean_var{n}", [P, TT, 2]) for n in (1, 2, 3)]
        var_eps = [None] + [sb(f"var_eps{n}", [P, TT]) for n in (1, 2, 3)]
        rstd = [None] + [sb(f"rstd{n}", [P, TT]) for n in (1, 2, 3)]
        row_sum = sb("row_sum", [P, TT])
        minus_mean = sb("minus_mean", [P, TT])
        square_sum = sb("square_sum", [P, TT])
        unread = sb("unread", [P, 2, TT, C])
        shift = [None] + [sb(f"shift{n}", [P, TT]) for n in (1, 2, 3)]

        z_high = [None, sb("z_high1", [P, CH, T], f16), None, sb("z_high3", [P, CH, T], f16)]
        z_low = [None, sb("z_low1", [P, CH, T], f16), None, sb("z_low3", [P, CH, T], f16)]
        XM = sb("XM", [P, 2, CH, T])
        EK = sb("EK", [P, 2, CH, T])
        KV = sb("KV", [P, 2, CH, T])
        TH = sb("TH", [P, 2, CH, T])
        FK = sb("FK", [P, 2, CH, T])
        SK = sb("SK", [P, 2, CH, T + 1])
        SV = sb("SV", [P, 2, CH, T + 1])
        WK = sb("WK", [P, 2, CH, T])
        WV = sb("WV", [P, 2, CH, T])
        Y0 = sb("Y0", [P, 2, CH, T])
        SS = sb("SS", [P, 2, CH, T])
        QQ = sb("QQ", [P, 2, CH, T])
        F = sb("F", [P, 2, CH, T])

        banks = [ctx.enter_context(nc.psum_tensor(f"bank{i}", [P, T], f32)) for i in range(8)]
        turned = banks[0:2]
        tokens = banks[2:4]
        ring = banks[4:8]

        x_loaded = [sem(f"x_loaded{i}") for i in range(2)]
        weights_loaded = sem("weights_loaded")
        vectors_loaded = sem("vectors_loaded")
        ffn_loaded = sem("ffn_loaded")
        x1_held = [sem(f"x1_held{i}") for i in range(2)]
        out_stored = [sem(f"out_stored{i}") for i in range(2)]
        gpsimd_consts = sem("gpsimd_consts")
        warm_filled = sem("warm_filled")
        dve_consts = sem("dve_consts")
        dve_ones = sem("dve_ones")
        act_vectors = sem("act_vectors")
        act_decay = sem("act_decay")
        abs_summed = sem("abs_summed")
        scale_summed = sem("scale_summed")
        scale_ready = sem("scale_ready")
        below_ready = sem("below_ready")
        ternary_ready = sem("ternary_ready")
        stats_ready = [None] + [sem(f"stats_ready{n}") for n in (1, 2, 3)]
        mean_ready = [None] + [sem(f"mean_ready{n}") for n in (1, 2, 3)]
        var_ready = [None] + [sem(f"var_ready{n}") for n in (1, 2, 3)]
        rstd_ready = [None] + [sem(f"rstd_ready{n}") for n in (1, 2, 3)]
        shift_ready = [None] + [sem(f"shift_ready{n}") for n in (1, 2, 3)]
        z_ready = [None] + [sem(f"z_ready{n}") for n in (1, 2, 3)]
        turned_ready = [None] + [sem(f"turned_ready{n}") for n in (1, 2, 3)]
        row_sum_ready = sem("row_sum_ready")
        minus_mean_ready = sem("minus_mean_ready")
        square_sum_ready = sem("square_sum_ready")
        high_ready = [None, sem("high_ready1"), None, sem("high_ready3")]
        low_ready = [None, sem("low_ready1"), None, sem("low_ready3")]
        product_ready = [None, sem("ffn1_ready"), sem("wo_ready"), sem("ffn3_ready")]
        x_ready = [None] + [sem(f"x{n}_ready") for n in (1, 2, 3)]
        scaled_ready = sem("scaled_ready")
        mixed_ready = sem("mixed_ready")
        k_ready, v_ready, r_ready = sem("k_ready"), sem("v_ready"), sem("r_ready")
        exp_k_ready = sem("exp_k_ready")
        tanh_ready = sem("tanh_ready")
        kv_ready = sem("kv_ready")
        clamped_ready = sem("clamped_ready")
        k_state_ready = sem("k_state_ready")
        v_state_ready = sem("v_state_ready")
        first_k_ready = sem("first_k_ready")
        wk_ready = sem("wk_ready")
        wv_ready = sem("wv_ready")
        gated_ready = sem("gated_ready")
        guess_ready = sem("guess_ready")
        s_ready = sem("s_ready")
        guessed_ready = sem("guessed_ready")
        square_ready = sem("square_ready")
        linear_ready = sem("linear_ready")
        rwkv_ready = sem("rwkv_ready")

        def run_steps(engine, last_lag, step):
            loop_from = 4
            loop_to = SEQS - (SEQS - loop_from) % 2
            for t in range(loop_from):
                step(t, t % 2, lambda lag: 0 <= t - lag < SEQS)
            with engine.Fori(loop_from, loop_to - 1, 2) as t:
                step(t, 0, lambda lag: True)
                step(t + 1, 1, lambda lag: True)
            for t in range(loop_to, SEQS + last_lag):
                step(t, t % 2, lambda lag: 0 <= t - lag < SEQS)

        def beyond(b, n):
            return not isinstance(b, int) or b >= n

        def by_vector(n, b):
            return isinstance(b, int) and b in (NORM_FIRST if n < 3 else NORM_LAST)

        block = ctx.enter_context(nc.Block())

        @block.sync
        def _(sp):
            def load(b, p):
                if beyond(b, 2):
                    sp.wait_ge(x_ready[1], 2 * (b - 1))
                sp.dma_start(X0[:, p], x_dram[bass.ds(b, 1)].rearrange("s p j c -> p (s j) c")
                             if not isinstance(b, int) else x_dram[b]).then_inc(x_loaded[p], 16)

            def hold(b, p):
                sp.wait_ge(x_ready[1], 2 * (b + 1))
                if beyond(b, 2):
                    sp.wait_ge(x_ready[2], 2 * (b - 1))
                sp.dma_start(X1_held[:, p], X1[:, p]).then_inc(x1_held[p], 16)

            def store(b, p):
                sp.wait_ge(x_ready[3], 2 * (b + 1))
                sp.dma_start(out_dram[bass.ds(b, 1)].rearrange("s p j c -> p (s j) c")
                             if not isinstance(b, int) else out_dram[b], X3[:, p]).then_inc(out_stored[p], 16)

            load(0, 0)
            sp.dma_start(w_f[:, :, :], ffn_t.rearrange("(k p) o -> p k o", p=P)).then_inc(ffn_loaded, 16)
            for vec, dram in ((decay_in, time_decay), (first_in, time_first), (mix, time_mix)):
                sp.dma_start(vec[:, :], dram).then_inc(vectors_loaded, 16)
            for w, dram in ((w_k, wk_t), (w_v, wv_t), (w_r, wr_t), (w_o, wo_t)):
                sp.dma_start(w[:, :, :], dram.rearrange("(k p) o -> p k o", p=P)).then_inc(weights_loaded, 16)
            load(1, 1)

            def step(t, u, has):
                if has(0) and beyond(t, 2):
                    load(t, u)
                if has(1):
                    hold(t - 1, (u + 1) % 2)
                if has(4):
                    store(t - 4, (u + 4) % 2)

            run_steps(sp, 4, step)
            for stored in out_stored:
                sp.wait_ge(stored, 8 * SEQS + 1)

        @block.gpsimd
        def _(pool):
            nc.gpsimd.memset(ident[:, :], 0.0).then_inc(gpsimd_consts, 1)
            nc.gpsimd.memset(half_power[:, :], -0.5).then_inc(gpsimd_consts, 1)
            nc.gpsimd.memset(warm[:, :], 1.0).then_inc(warm_filled, 1)
            pool.wait_ge(gpsimd_consts, 2)
            nc.gpsimd.affine_select(out=ident[:, :], in_=ident[:, :], compare_op=ALU.not_equal, fill=1.0,
                                    base=0, pattern=[[-1, P]], channel_multiplier=1).then_inc(gpsimd_consts, 1)

            def inverse_std(n, b, p):
                pool.wait_ge(var_ready[n], b + 1)
                if beyond(b, 1):
                    pool.wait_ge(z_ready[n], TT * b)
                nc.gpsimd.tensor_tensor(rstd[n][:, :], var_eps[n][:, :], half_power[:, :],
                                        ALU.pow).then_inc(rstd_ready[n], 1)

            def denominator(b, p, m):
                pool.wait_ge(first_k_ready, CH * b + m + 1)
                pool.wait_ge(k_state_ready, CH * b + m + 1)
                if beyond(b, 2):
                    pool.wait_ge(guess_ready, CH * (b - 1))
                nc.gpsimd.tensor_tensor(WK[:, p, m], FK[:, p, m], SK[:, p, m, 0:T], ALU.add).then_inc(wk_ready, 1)

            def times_guess(b, p, m):
                pool.wait_ge(guess_ready, CH * b + m + 1)
                if beyond(b, 2):
                    pool.wait_ge(linear_ready, CH * (b - 1))
                    pool.wait_ge(square_ready, CH * (b - 1))
                nc.gpsimd.tensor_tensor(SS[:, p, m], WK[:, p, m], Y0[:, p, m], ALU.mult).then_inc(s_ready, 1)

            def numerator_times_guess(b, p, m):
                pool.wait_ge(gated_ready, CH * b + m + 1)
                pool.wait_ge(guess_ready, CH * b + m + 1)
                nc.gpsimd.tensor_tensor(WV[:, p, m], WV[:, p, m], Y0[:, p, m],
                                        ALU.mult).then_inc(guessed_ready, 1)

            def step(t, u, has):
                if has(0):
                    inverse_std(1, t, u)
                if has(2):
                    numerator_times_guess(t - 2, (u + 2) % 2, 0)
                if has(3):
                    inverse_std(3, t - 3, (u + 3) % 2)
                if has(2):
                    times_guess(t - 2, (u + 2) % 2, 1)
                    numerator_times_guess(t - 2, (u + 2) % 2, 1)
                if has(0):
                    inverse_std(2, t, u)
                if has(1):
                    denominator(t - 1, (u + 1) % 2, 0)
                    times_guess(t - 1, (u + 1) % 2, 0)
                    denominator(t - 1, (u + 1) % 2, 1)

            run_steps(pool, 3, step)

        @block.scalar
        def _(act):
            act.wait_ge(vectors_loaded, 48)
            nc.scalar.activation(decay_exp[:, :], decay_in[:, :], ACT.Exp).then_inc(act_vectors, 1)
            nc.scalar.activation(first_w[:, :], first_in[:, :], ACT.Exp).then_inc(act_vectors, 1)
            act.wait_ge(act_vectors, 2)
            nc.scalar.activation(decay[:, :], decay_exp[:, :], ACT.Exp, scale=-1.0).then_inc(act_decay, 1)
            act.wait_ge(ffn_loaded, 16)
            nc.scalar.activation(w_abs[:, :, :], w_f[:, :, :], ACT.Abs,
                                 accum_out=abs_sum[:, :]).then_inc(abs_summed, 1)

            def normalize(n, b, p):
                if by_vector(n, b):
                    return
                act.wait_ge(shift_ready[n], b + 1 - (len(NORM_FIRST) if n < 3 else 0))
                if beyond(b, 1):
                    act.wait_ge(turned_ready[n], b)
                for j in range(TT):
                    nc.scalar.activation(Z[n][:, j], XS[n - 1][:, p, j], ACT.Identity, bias=shift[n][:, j:j + 1],
                                         scale=rstd[n][:, j:j + 1]).then_inc(z_ready[n], 1)

            def sum_rows(b, p, j):
                if by_vector(3, b):
                    return
                act.wait_ge(x_ready[3 - 1], 2 * b + j // 2 + 1)
                if beyond(b, 1):
                    act.wait_ge(minus_mean_ready, b)
                nc.scalar.activation(unread[:, 0, j], XS[3 - 1][:, p, j], ACT.Copy,
                                     accum_out=row_sum[:, j:j + 1]).then_inc(row_sum_ready, 1)

            def sum_squares(b, p, j):
                if by_vector(3, b):
                    return
                act.wait_ge(minus_mean_ready, b + 1)
                if beyond(b, 1):
                    act.wait_ge(var_ready[3], b)
                nc.scalar.activation(unread[:, 1, j], XS[3 - 1][:, p, j], ACT.Square, bias=minus_mean[:, j:j + 1],
                                     accum_out=square_sum[:, j:j + 1]).then_inc(square_sum_ready, 1)

            def high_half(n, b, p, m):
                act.wait_ge(turned_ready[n], b + 1)
                if beyond(b, 1):
                    act.wait_ge(product_ready[n], 2 * b)
                nc.scalar.activation(z_high[n][:, m], turned[m][:, :], ACT.Copy).then_inc(high_ready[n], 1)

            def scale_mix(b, p, m):
                act.wait_ge(turned_ready[2], b + 1)
                if beyond(b, 2):
                    act.wait_ge(r_ready, CH * (b - 1))
                nc.scalar.activation(XM[:, p, m], turned[m][:, :], ACT.Identity,
                                     scale=mix[:, m:m + 1]).then_inc(scaled_ready, 1)

            def clamp_k(b, p, m):
                act.wait_ge(k_ready, CH * b + m + 1)
                k = ring[(2 * p + 3 * m) % 4][:, :]
                nc.scalar.activation(k, k, ACT.Relu, scale=-1.0, bias=K_CLAMP).then_inc(clamped_ready, 1)

            def exp_k(b, p, m):
                act.wait_ge(clamped_ready, CH * b + m + 1)
                if beyond(b, 2):
                    act.wait_ge(k_state_ready, CH * (b - 1))
                    act.wait_ge(kv_ready, CH * (b - 1))
                nc.scalar.activation(EK[:, p, m], ring[(2 * p + 3 * m) % 4][:, :], ACT.Exp, scale=-1.0,
                                     bias=K_CLAMP).then_inc(exp_k_ready, 1)

            def first_k(b, p, m):
                act.wait_ge(exp_k_ready, CH * b + m + 1)
                if beyond(b, 2):
                    act.wait_ge(wk_ready, CH * (b - 1))
                nc.scalar.activation(FK[:, p, m], EK[:, p, m], ACT.Identity, scale=first_w[:, m:m + 1],
                                     bias=WKV_EPS).then_inc(first_k_ready, 1)

            def tanh_r(b, p, m):
                act.wait_ge(r_ready, CH * b + m + 1)
                if beyond(b, 2):
                    act.wait_ge(gated_ready, CH * (b - 1))
                nc.scalar.activation(TH[:, p, m], ring[(2 * p + 3 * m + 2) % 4][:, :], ACT.Tanh,
                                     scale=-0.5).then_inc(tanh_ready, 1)

            def guess(b, p, m):
                act.wait_ge(wk_ready, CH * b + m + 1)
                if beyond(b, 2):
                    act.wait_ge(s_ready, CH * (b - 1))
                    act.wait_ge(guessed_ready, CH * (b - 1))
                nc.scalar.activation(Y0[:, p, m], WK[:, p, m].bitcast(i32), ACT.Exp, scale=RC["guess_scale"],
                                     bias=RC["guess_bias"]).then_inc(guess_ready, 1)

            def square(b, p, m):
                act.wait_ge(s_ready, CH * b + m + 1)
                if beyond(b, 2):
                    act.wait_ge(rwkv_ready, CH * (b - 1))
                nc.scalar.activation(QQ[:, p, m], SS[:, p, m], ACT.Square,
                                     scale=RC["square_scale"], bias=RC["square_bias"]).then_inc(square_ready, 1)

            def step(t, u, has):
                if has(0):
                    normalize(1, t, u)
                if has(3):
                    sum_squares(t - 3, (u + 3) % 2, 2)
                    sum_squares(t - 3, (u + 3) % 2, 3)
                if has(0):
                    high_half(1, t, u, 0)
                    high_half(1, t, u, 1)
                if has(2):
                    tanh_r(t - 2, (u + 2) % 2, 1)
                if has(1):
                    clamp_k(t - 1, (u + 1) % 2, 0)
                    exp_k(t - 1, (u + 1) % 2, 0)
                if has(2):
                    guess(t - 2, (u + 2) % 2, 1)
                if has(3):
                    normalize(3, t - 3, (u + 3) % 2)
                if has(1):
                    first_k(t - 1, (u + 1) % 2, 0)
                if has(3):
                    high_half(3, t - 3, (u + 3) % 2, 0)
                    high_half(3, t - 3, (u + 3) % 2, 1)
                if has(2):
                    square(t - 2, (u + 2) % 2, 1)
                if has(1):
                    tanh_r(t - 1, (u + 1) % 2, 0)
                    clamp_k(t - 1, (u + 1) % 2, 1)
                    exp_k(t - 1, (u + 1) % 2, 1)
                if has(0):
                    normalize(2, t, u)
                if has(1):
                    first_k(t - 1, (u + 1) % 2, 1)
                    guess(t - 1, (u + 1) % 2, 0)
                if has(2):
                    sum_rows(t - 2, (u + 2) % 2, 0)
                    sum_rows(t - 2, (u + 2) % 2, 1)
                if has(0):
                    scale_mix(t, u, 0)
                if has(2):
                    sum_rows(t - 2, (u + 2) % 2, 2)
                    sum_rows(t - 2, (u + 2) % 2, 3)
                if has(0):
                    scale_mix(t, u, 1)
                if has(1):
                    square(t - 1, (u + 1) % 2, 0)
                if has(2):
                    sum_squares(t - 2, (u + 2) % 2, 0)
                    sum_squares(t - 2, (u + 2) % 2, 1)

            run_steps(act, 3, step)

        @block.vector
        def _(dve):
            nc.vector.memset(ones[:, :], 1.0).then_inc(dve_ones, 1)
            nc.vector.memset(decay_rows[:, :, :], 1.0).then_inc(dve_consts, 1)
            for parity, stored in enumerate(out_stored):
                nc.vector.memset(X3[:, parity, 0, 0:1], 0.0).then_inc(stored, 1)
            for state in (SK, SV):
                nc.vector.memset(state[:, :, :, 0:1], 0.0).then_inc(dve_consts, 1)

            def spread_decay():
                dve.wait_ge(act_decay, 1)
                dve.wait_ge(dve_consts, 3)
                for m in range(CH):
                    nc.vector.tensor_scalar(decay_rows[:, m], decay_rows[:, m], decay[:, m:m + 1], None,
                                            ALU.mult).then_inc(dve_consts, 1)
                nc.vector.tensor_scalar(mix_rest[:, :], mix[:, :], -1.0, 1.0, ALU.mult, ALU.add).then_inc(dve_consts, 1)

            def quantize():
                dve.wait_ge(scale_summed, 1)
                nc.vector.tensor_scalar(half_scale[:, :], tokens[0][:, 0:1], 0.5 / (C * C), 0.5 * QUANT_EPS, ALU.mult,
                                        ALU.max).then_inc(scale_ready, 1)
                dve.wait_ge(scale_ready, 1)
                nc.vector.tensor_scalar(minus_half_scale[:, :], half_scale[:, :], -1.0, None,
                                        ALU.mult).then_inc(scale_ready, 1)
                dve.wait_ge(scale_ready, 2)
                nc.vector.tensor_scalar(w_below[:, :, :], w_f[:, :, :], minus_half_scale[:, :], None,
                                        ALU.is_lt).then_inc(below_ready, 1)
                dve.wait_ge(below_ready, 1)
                nc.vector.scalar_tensor_tensor(ternary[:, :, :], w_f[:, :, :], half_scale[:, :], w_below[:, :, :],
                                               ALU.is_gt, ALU.subtract).then_inc(ternary_ready, 1)

            def stats(n, b, p, j):
                if n == 1:
                    dve.wait_ge(x_loaded[p], 8 * (b - p) + 16)
                else:
                    dve.wait_ge(x_ready[n - 1], 2 * b + j // 2 + 1)
                nc.vector.bn_stats(bn[n][:, j], XS[n - 1][:, p, j]).then_inc(stats_ready[n], 1)

            def variance(n, b, p):
                dve.wait_ge(stats_ready[n], TT * (b + 1) if n < 3 else TT * (b + 1 - SEQS + len(NORM_LAST)))
                dve.nop(nofuse=True)
                for j in range(TT):
                    nc.vector.bn_aggr(mean_var[n][:, j], bn[n][:, j]).then_inc(mean_ready[n], 1)
                dve.wait_ge(mean_ready[n], TT * (b + 1) if n < 3 else TT * (b + 1 - SEQS + len(NORM_LAST)))
                if beyond(b, 1):
                    dve.wait_ge(rstd_ready[n], b)
                nc.vector.tensor_scalar(var_eps[n][:, :], mean_var[n][:, :, 1], LN_EPS, None,
                                        ALU.add).then_inc(var_ready[n], 1)

            def negate_mean(b, p):
                if by_vector(3, b):
                    return
                dve.wait_ge(row_sum_ready, TT * (b + 1))
                if beyond(b, 1):
                    dve.wait_ge(square_sum_ready, TT * b)
                nc.vector.tensor_scalar(minus_mean[:, :], row_sum[:, :], -1.0 / C, None,
                                        ALU.mult).then_inc(minus_mean_ready, 1)

            def variance_of_squares(b, p):
                if by_vector(3, b):
                    for j in range(TT):
                        stats(3, b, p, j)
                    variance(3, b, p)
                    return
                dve.wait_ge(square_sum_ready, TT * (b + 1))
                if beyond(b, 1):
                    dve.wait_ge(rstd_ready[3], b)
                nc.vector.tensor_scalar(var_eps[3][:, :], square_sum[:, :], 1.0 / C, LN_EPS, ALU.mult,
                                        ALU.add).then_inc(var_ready[3], 1)

            def shifts(n, b, p):
                if n == 1 and isinstance(b, int) and b == 0:
                    quantize()
                dve.wait_ge(rstd_ready[n], b + 1)
                if by_vector(n, b):
                    if b:
                        dve.wait_ge(turned_ready[n], b)
                    for j in range(TT):
                        nc.vector.tensor_scalar(Z[n][:, j], XS[n - 1][:, p, j], mean_var[n][:, j, 0:1],
                                                rstd[n][:, j:j + 1], ALU.subtract, ALU.mult).then_inc(z_ready[n], 1)
                    return
                if beyond(b, 1):
                    dve.wait_ge(z_ready[n], TT * b)
                if n == 3:
                    dve.wait_ge(minus_mean_ready, b + 1)
                    nc.vector.tensor_tensor(shift[n][:, :], minus_mean[:, :], rstd[n][:, :],
                                            ALU.mult).then_inc(shift_ready[n], 1)
                else:
                    nc.vector.scalar_tensor_tensor(shift[n][:, :], mean_var[n][:, :, 0], -1.0, rstd[n][:, :],
                                                   ALU.mult, ALU.mult).then_inc(shift_ready[n], 1)

            def low_half(n, b, p, m):
                dve.wait_ge(high_ready[n], CH * b + m + 1)
                if beyond(b, 1):
                    dve.wait_ge(product_ready[n], 2 * b)
                nc.vector.tensor_tensor(z_low[n][:, m], turned[m][:, :], z_high[n][:, m],
                                        ALU.subtract).then_inc(low_ready[n], 1)

            def residual(n, b, p, h):
                if n == 1 and h == 0 and isinstance(b, int) and b == 0:
                    spread_decay()
                dve.wait_ge(product_ready[n], 2 * b + h + 1)
                if n == 1:
                    dve.wait_ge(z_ready[1], TT * (b + 1))
                if n == 3 and beyond(b, 2):
                    dve.wait_ge(out_stored[p], 8 * (b - p) + 1)
                if n == 1 and beyond(b, 2):
                    dve.wait_ge(z_ready[2], TT * (b - 1))
                    dve.wait_ge(x1_held[p], 8 * (b - p))
                if n == 2:
                    dve.wait_ge(x1_held[p], 8 * (b - p) + 16)
                    if beyond(b, 2):
                        dve.wait_ge(z_ready[3], TT * (b - 1))
                        dve.wait_ge(x_ready[3], 2 * (b - 1))
                old = (X1_held if n == 2 else XS[n - 1])[:, p, 2 * h:2 * h + 2]
                new = XS[n][:, p, 2 * h:2 * h + 2]
                bank = tokens[h][:, :].rearrange("p (j c) -> p j c", c=C)
                if n == 2:
                    nc.vector.tensor_tensor(new, bank, old, ALU.add).then_inc(x_ready[n], 1)
                else:
                    nc.vector.scalar_tensor_tensor(new, bank, half_scale[:, :], old, ALU.mult,
                                                   ALU.add).then_inc(x_ready[n], 1)

            def token_mix(b, p, m):
                if m == 0 and isinstance(b, int) and b == 0:
                    dve.wait_ge(dve_consts, DVE_CONSTS)
                dve.wait_ge(scaled_ready, CH * b + m + 1)
                nc.vector.scalar_tensor_tensor(XM[:, p, m, 1:T], turned[m][:, 0:T - 1], mix_rest[:, m:m + 1],
                                               XM[:, p, m, 1:T], ALU.mult, ALU.add).then_inc(mixed_ready, 1)

            def key_value(b, p, m):
                dve.wait_ge(exp_k_ready, CH * b + m + 1)
                dve.wait_ge(v_ready, CH * b + m + 1)
                nc.vector.tensor_tensor(KV[:, p, m], EK[:, p, m], ring[(2 * p + 3 * m + 1) % 4][:, :],
                                        ALU.mult).then_inc(kv_ready, 1)

            def k_state(b, p, m):
                dve.wait_ge(exp_k_ready, CH * b + m + 1)
                if beyond(b, 2):
                    dve.wait_ge(wk_ready, CH * (b - 1))
                nc.vector.tensor_tensor_scan(SK[:, p, m, 1:T + 1], decay_rows[:, m], EK[:, p, m], 0.0, ALU.mult,
                                             ALU.add).then_inc(k_state_ready, 1)

            def v_state(b, p, m):
                dve.wait_ge(kv_ready, CH * b + m + 1)
                nc.vector.tensor_tensor_scan(SV[:, p, m, 1:T + 1], decay_rows[:, m], KV[:, p, m], 0.0, ALU.mult,
                                             ALU.add).then_inc(v_state_ready, 1)

            def numerator(b, p, m):
                dve.wait_ge(v_state_ready, CH * b + m + 1)
                nc.vector.scalar_tensor_tensor(WV[:, p, m], KV[:, p, m], first_w[:, m:m + 1], SV[:, p, m, 0:T],
                                               ALU.mult, ALU.add).then_inc(wv_ready, 1)

            def gate(b, p, m):
                dve.wait_ge(tanh_ready, CH * b + m + 1)
                dve.wait_ge(wv_ready, CH * b + m + 1)
                nc.vector.scalar_tensor_tensor(WV[:, p, m], TH[:, p, m], -1.0, WV[:, p, m], ALU.add,
                                               ALU.mult).then_inc(gated_ready, 1)

            def linear(b, p, m):
                dve.wait_ge(guessed_ready, CH * b + m + 1)
                dve.wait_ge(s_ready, CH * b + m + 1)
                nc.vector.scalar_tensor_tensor(WV[:, p, m], SS[:, p, m], -RC["root"], WV[:, p, m], ALU.add,
                                               ALU.mult).then_inc(linear_ready, 1)

            def rwkv(b, p, m):
                dve.wait_ge(square_ready, CH * b + m + 1)
                dve.wait_ge(linear_ready, CH * b + m + 1)
                if beyond(b, 2):
                    dve.wait_ge(product_ready[2], 2 * (b - 1))
                nc.vector.scalar_tensor_tensor(F[:, p, m], QQ[:, p, m], RC["rest"], WV[:, p, m], ALU.add,
                                               ALU.mult).then_inc(rwkv_ready, 1)

            def step(t, u, has):
                if has(0):
                    stats(1, t, u, 0)
                    stats(1, t, u, 1)
                    stats(1, t, u, 2)
                    stats(1, t, u, 3)
                    variance(1, t, u)
                if has(3):
                    negate_mean(t - 3, (u + 3) % 2)
                if has(1):
                    token_mix(t - 1, (u + 1) % 2, 0)
                    token_mix(t - 1, (u + 1) % 2, 1)
                if has(0):
                    shifts(1, t, u)
                if has(2):
                    key_value(t - 2, (u + 2) % 2, 1)
                    v_state(t - 2, (u + 2) % 2, 1)
                    linear(t - 2, (u + 2) % 2, 0)
                    numerator(t - 2, (u + 2) % 2, 1)
                if has(3):
                    variance_of_squares(t - 3, (u + 3) % 2)
                if has(2):
                    rwkv(t - 2, (u + 2) % 2, 0)
                if has(0):
                    low_half(1, t, u, 0)
                    low_half(1, t, u, 1)
                if has(3):
                    shifts(3, t - 3, (u + 3) % 2)
                if has(2):
                    gate(t - 2, (u + 2) % 2, 1)
                if has(1):
                    key_value(t - 1, (u + 1) % 2, 0)
                if has(0):
                    residual(1, t, u, 0)
                    residual(1, t, u, 1)
                    stats(2, t, u, 0)
                    stats(2, t, u, 1)
                    stats(2, t, u, 2)
                    stats(2, t, u, 3)
                    variance(2, t, u)
                if has(2):
                    linear(t - 2, (u + 2) % 2, 1)
                if has(3):
                    low_half(3, t - 3, (u + 3) % 2, 0)
                    low_half(3, t - 3, (u + 3) % 2, 1)
                if has(2):
                    rwkv(t - 2, (u + 2) % 2, 1)
                if has(1):
                    k_state(t - 1, (u + 1) % 2, 0)
                if has(3):
                    residual(3, t - 3, (u + 3) % 2, 0)
                if has(0):
                    shifts(2, t, u)
                if has(3):
                    residual(3, t - 3, (u + 3) % 2, 1)
                if has(1):
                    v_state(t - 1, (u + 1) % 2, 0)
                    k_state(t - 1, (u + 1) % 2, 1)
                    numerator(t - 1, (u + 1) % 2, 0)
                if has(2):
                    residual(2, t - 2, (u + 2) % 2, 0)
                if has(1):
                    gate(t - 1, (u + 1) % 2, 0)
                if has(2):
                    residual(2, t - 2, (u + 2) % 2, 1)

            run_steps(dve, 3, step)

        @block.tensor
        def _(pe):
            pe.wait_ge(dve_ones, 1)
            pe.wait_ge(abs_summed, 1)
            nc.tensor.matmul(tokens[0][:, 0:1], ones[:, :], abs_sum[:, :], start=True, stop=True).then_inc(scale_summed, 1)
            pe.wait_ge(gpsimd_consts, 3)

            def warm_up(count, bank):
                for _ in range(count):
                    nc.tensor.matmul(bank[:, :], warm[:, 0:P], warm[:, :], start=True, stop=True)

            def bank_free(readers, per_batch, b, upto):
                if isinstance(b, int):
                    if b < 0:
                        return
                    b = min(b, SEQS - 1)
                pe.wait_ge(readers, per_batch * b + upto)

            def turn(n, b, p, after):
                if n == 2 and isinstance(b, int) and b == 0:
                    warm_up(WARM[1], ring[3])
                if n == 3 and isinstance(b, int) and b >= SEQS - 2:
                    pe.wait_ge(tanh_ready, CH * SEQS - 1)
                    warm_up(WARM[3 + b - SEQS + 2], ring[0])
                for m, last_b in after.items():
                    bank_free(mixed_ready if m == 2 else low_ready[m], CH, last_b, CH)
                for j in range(TT):
                    pe.wait_ge(z_ready[n], TT * b + j + 1)
                    for m in range(CH):
                        last = nc.tensor.transpose(turned[m][:, j * P:(j + 1) * P], Z[n][:, j, m * P:(m + 1) * P],
                                                   ident[:, :])
                last.then_inc(turned_ready[n], 1)

            def ffn(n, b, p, h, after):
                for m, last_b in after.items():
                    bank_free(x_ready[m], 2, last_b, h + 1)
                if n == 1 and isinstance(b, int) and b == 0:
                    pe.wait_ge(ternary_ready, 1)
                if n == 3 and h == 0 and isinstance(b, int) and b >= SEQS - 2:
                    warm_up(WARM[5], ring[0])
                pe.wait_ge(low_ready[n], CH * (b + 1))
                for j in (2 * h, 2 * h + 1):
                    o = tokens[h][:, (j % 2) * C:(j % 2 + 1) * C]
                    parts = [(part, m) for m in range(CH) for part in (z_high[n], z_low[n])]
                    for i, (part, m) in enumerate(parts):
                        last = nc.tensor.matmul(o, part[:, m, j * P:(j + 1) * P], ternary[:, m],
                                                start=i == 0, stop=i == len(parts) - 1)
                last.then_inc(product_ready[n], 1)

            def output_product(b, p, h, after):
                for m, last_b in after.items():
                    bank_free(x_ready[m], 2, last_b, h + 1)
                pe.wait_ge(rwkv_ready, CH * (b + 1))
                for j in (2 * h, 2 * h + 1):
                    o = tokens[h][:, (j % 2) * C:(j % 2 + 1) * C]
                    for m in range(CH):
                        last = nc.tensor.matmul(o, F[:, p, m, j * P:(j + 1) * P], w_o[:, m],
                                                start=m == 0, stop=m == CH - 1)
                last.then_inc(product_ready[2], 1)

            def project(b, p, w, use, ready, readers, b_before, m_before, m):
                if isinstance(b, int) and b == 0 and w is w_k and m == 0:
                    warm_up(WARM[2], ring[3])
                if beyond(b, 1) or b_before is b:
                    pe.wait_ge(readers, CH * b_before + m_before + 1)
                pe.wait_ge(mixed_ready, CH * (b + 1))
                if isinstance(b, int) and b == 0:
                    pe.wait_ge(weights_loaded, 64)
                for c in range(CH):
                    last = nc.tensor.matmul(ring[(2 * p + use) % 4][:, :], w[:, c, m * P:(m + 1) * P], XM[:, p, c],
                                            start=c == 0, stop=c == CH - 1)
                last.then_inc(ready, 1)

            def project_k(b, p, m):
                if m == 0:
                    project(b, p, w_k, 0, k_ready, tanh_ready, b - 1, 0, m)
                else:
                    project(b, p, w_k, 3, k_ready, tanh_ready, b - 1, 1, m)

            def project_v(b, p, m):
                if m == 0:
                    project(b, p, w_v, 1, v_ready, exp_k_ready, b - 1, 1, m)
                else:
                    project(b, p, w_v, 4, v_ready, exp_k_ready, b, 0, m)

            def project_r(b, p, m):
                if m == 0:
                    project(b, p, w_r, 2, r_ready, kv_ready, b - 1, 1, m)
                else:
                    project(b, p, w_r, 5, r_ready, kv_ready, b, 0, m)

            pe.wait_ge(warm_filled, 1)
            warm_up(WARM[0], ring[3])
            def step(t, u, has):
                if has(3):
                    output_product(t - 3, (u + 3) % 2, 1, after={1: t - 1, 2: t - 4, 3: t - 4})
                if has(1):
                    turn(2, t - 1, (u + 1) % 2, after={1: t - 1, 2: t - 2, 3: t - 4})
                if has(2):
                    project_v(t - 2, (u + 2) % 2, 1)
                    project_r(t - 2, (u + 2) % 2, 1)
                if has(1):
                    project_k(t - 1, (u + 1) % 2, 0)
                if has(0):
                    turn(1, t, u, after={1: t - 1, 2: t - 1, 3: t - 4})
                if has(1):
                    project_v(t - 1, (u + 1) % 2, 0)
                if has(0):
                    ffn(1, t, u, 0, after={1: t - 1, 2: t - 3, 3: t - 4})
                    ffn(1, t, u, 1, after={1: t - 1, 2: t - 3, 3: t - 4})
                if has(1):
                    project_r(t - 1, (u + 1) % 2, 0)
                if has(3):
                    turn(3, t - 3, (u + 3) % 2, after={1: t, 2: t - 1, 3: t - 4})
                if has(1):
                    project_k(t - 1, (u + 1) % 2, 1)
                if has(3):
                    ffn(3, t - 3, (u + 3) % 2, 0, after={1: t, 2: t - 3, 3: t - 4})
                    ffn(3, t - 3, (u + 3) % 2, 1, after={1: t, 2: t - 3, 3: t - 4})
                if has(2):
                    output_product(t - 2, (u + 2) % 2, 0, after={1: t, 2: t - 3, 3: t - 3})

            run_steps(pe, 3, step)


_OUT = "out"


def kernel(L0_attn_x, L0_attn_time_decay, L0_attn_time_first, L0_attn_time_mix, L0_attn_Wk, L0_attn_Wv, L0_attn_Wr,
           L0_attn_Wo, L0_ffn_weight):
    import concourse.bacc as bacc
    from concourse.bass_utils import run_bass_kernel_spmd

    def turned(w):
        return np.ascontiguousarray(np.asarray(w).T)

    def by_partition(v):
        return np.ascontiguousarray(np.asarray(v).reshape(-1, P).T)

    arrays = {
        "x": np.ascontiguousarray(L0_attn_x),
        "time_decay": by_partition(L0_attn_time_decay),
        "time_first": by_partition(L0_attn_time_first),
        "time_mix": by_partition(L0_attn_time_mix),
        "wk_t": turned(L0_attn_Wk),
        "wv_t": turned(L0_attn_Wv),
        "wr_t": turned(L0_attn_Wr),
        "wo_t": turned(L0_attn_Wo),
        "ffn_t": turned(L0_ffn_weight),
    }
    nc = bacc.Bacc("TRN2", target_bir_lowering=False, num_devices=1)
    args = [nc.dram_tensor(name, a.shape, mybir.dt.from_np(a.dtype), kind="ExternalInput").ap()
            for name, a in arrays.items()]
    x_shape = arrays["x"].shape
    out = nc.dram_tensor(_OUT, x_shape, mybir.dt.float32, kind="ExternalOutput").ap()
    macaron(nc, *args, out)
    result = run_bass_kernel_spmd(nc, [arrays], core_ids=[0])
    return result.results[0][_OUT]
```

```python
from contextlib import ExitStack

import numpy as np
import concourse.bass as bass
from concourse import mybir

P = 128
LN_EPS = 1e-5
QUANT_EPS = 1e-5
WKV_EPS = 1e-16
K_CLAMP = 60.0
WARM_START, WARM_TURN, WARM_PROJECT, WARM_LAST_TURN, WARM_LAST_FFN = 12, 13, 12, 14, 7


def reciprocal_constants():
    m = 1.0 / np.log(2.0) - 1.0
    shift = (np.log2(1.0 + m) - m) / 2.0
    low, high = 2.0 ** -shift, 2.0 ** shift
    line = np.polynomial.Polynomial([-(low + high) / (high - low), 2.0 / (high - low)])
    t4 = 8 * line ** 4 - 8 * line ** 2 + 1
    cubic = (1 - t4 / t4(0.0)).coef[1:]
    roots = np.polynomial.Polynomial(cubic).roots()
    root = float(roots[np.argmin(np.abs(roots.imag))].real)
    pair = roots[np.argmax(roots.imag)]
    gain = float(-cubic[3]) / 2.0
    return {
        "guess_scale": float(-np.log(2.0) / 2.0 ** 23),
        "guess_bias": float((127.0 - shift) * np.log(2.0)),
        "root": root,
        "square_scale": gain ** 0.5,
        "square_bias": float(-pair.real) * gain ** 0.5,
        "rest": float(pair.imag ** 2) * gain,
    }


def macaron(nc, x, time_decay, time_first, time_mix, wk_t, wv_t, wr_t, wo_t, ffn_t, out):
    f32, f16, i32 = mybir.dt.float32, mybir.dt.float16, mybir.dt.int32
    ALU = mybir.AluOpType
    ACT = mybir.ActivationFunctionType

    SEQS, T, C = x.shape
    CH = C // P
    TT = T // P
    RC = reciprocal_constants()
    DVE_CONSTS = 3 + CH + 1

    x_dram = x.rearrange("s (j p) c -> s p j c", p=P)
    out_dram = out.rearrange("s (j p) c -> s p j c", p=P)

    ctx = ExitStack()
    with ctx:
        def sb(name, shape, dt=f32):
            return ctx.enter_context(nc.sbuf_tensor(name, shape, dt))

        def sem(name):
            return ctx.enter_context(nc.semaphore(name))

        ident = sb("ident", [P, P])
        ones = sb("ones", [P, P])
        warm = sb("warm", [P, T], f16)
        decay_rows = sb("decay_rows", [P, CH, T])
        decay_in = sb("decay_in", [P, CH])
        decay_exp = sb("decay_exp", [P, CH])
        decay = sb("decay", [P, CH])
        first_in = sb("first_in", [P, CH])
        first_w = sb("first_w", [P, CH])
        mix = sb("mix", [P, CH])
        mix_rest = sb("mix_rest", [P, CH])
        half_power = sb("half_power", [P, TT])
        w_k = sb("w_k", [P, CH, C])
        w_v = sb("w_v", [P, CH, C])
        w_r = sb("w_r", [P, CH, C])
        w_o = sb("w_o", [P, CH, C])
        w_f = sb("w_f", [P, CH, C])
        w_below = sb("w_below", [P, CH, C])
        w_abs = sb("w_abs", [P, CH, C])
        ternary = sb("ternary", [P, CH, C], f16)
        abs_sum = sb("abs_sum", [P, 1])
        half_scale = sb("half_scale", [P, 1])
        minus_half_scale = sb("minus_half_scale", [P, 1])

        X0 = sb("X0", [P, 2, TT, C])
        X1 = sb("X1", [P, 2, TT, C])
        X2 = sb("X2", [P, 2, TT, C])
        X3 = sb("X3", [P, 2, TT, C])
        X1_held = sb("X1_held", [P, 2, TT, C])
        XS = [X0, X1, X2, X3]
        Z = [None] + [sb(f"Z{n}", [P, TT, C]) for n in (1, 2, 3)]
        bn = [None] + [sb(f"bn{n}", [P, TT, 6]) for n in (1, 2, 3)]
        mean_var = [None] + [sb(f"mean_var{n}", [P, TT, 2]) for n in (1, 2, 3)]
        var_eps = [None] + [sb(f"var_eps{n}", [P, TT]) for n in (1, 2, 3)]
        rstd = [None] + [sb(f"rstd{n}", [P, TT]) for n in (1, 2, 3)]
        row_sum = [None, None] + [sb(f"row_sum{n}", [P, TT]) for n in (2, 3)]
        minus_mean = [None] + [sb(f"minus_mean{n}", [P, TT]) for n in (1, 2, 3)]
        square_sum = [None, None] + [sb(f"square_sum{n}", [P, TT]) for n in (2, 3)]
        shift = [None] + [sb(f"shift{n}", [P, TT]) for n in (1, 2, 3)]
        squares = sb("squares", [P, TT, C])

        z_high = [None, sb("z_high1", [P, CH, T], f16), None, sb("z_high3", [P, CH, T], f16)]
        z_low = [None, sb("z_low1", [P, CH, T], f16), None, sb("z_low3", [P, CH, T], f16)]
        XM = sb("XM", [P, 2, CH, T])
        EK = sb("EK", [P, 2, CH, T])
        KV = sb("KV", [P, 2, CH, T])
        TH = sb("TH", [P, 2, CH, T])
        FK = sb("FK", [P, 2, CH, T])
        SK = sb("SK", [P, 2, CH, T + 1])
        SV = sb("SV", [P, 2, CH, T + 1])
        WK = sb("WK", [P, 2, CH, T])
        WV = sb("WV", [P, 2, CH, T])
        Y0 = sb("Y0", [P, 2, CH, T])
        SS = sb("SS", [P, 2, CH, T])
        QQ = sb("QQ", [P, 2, CH, T])
        F = sb("F", [P, 2, CH, T])

        banks = [ctx.enter_context(nc.psum_tensor(f"bank{i}", [P, T], f32)) for i in range(8)]
        turned = banks[0:2]
        tokens = banks[2:4]
        ring = banks[4:8]

        RING = (("k", 0), ("v", 0), ("r", 0), ("k", 1), ("v", 1), ("r", 1))

        def ring_bank(p, kind, m):
            return ring[(len(RING) * p + RING.index((kind, m))) % len(ring)]

        x_loaded = [sem(f"x_loaded{i}") for i in range(2)]
        first_half_loaded = sem("first_half_loaded")
        weights_loaded = sem("weights_loaded")
        vectors_loaded = sem("vectors_loaded")
        ffn_loaded = sem("ffn_loaded")
        x1_held = [sem(f"x1_held{i}") for i in range(2)]
        out_stored = [sem(f"out_stored{i}") for i in range(2)]
        gpsimd_consts = sem("gpsimd_consts")
        warm_filled = sem("warm_filled")
        dve_consts = sem("dve_consts")
        dve_ones = sem("dve_ones")
        act_vectors = sem("act_vectors")
        act_decay = sem("act_decay")
        abs_summed = sem("abs_summed")
        scale_summed = sem("scale_summed")
        scale_ready = sem("scale_ready")
        below_ready = sem("below_ready")
        ternary_ready = sem("ternary_ready")
        stats_ready = [None] + [sem(f"stats_ready{n}") for n in (1, 2, 3)]
        mean_ready = [None] + [sem(f"mean_ready{n}") for n in (1, 2, 3)]
        var_ready = [None] + [sem(f"var_ready{n}") for n in (1, 2, 3)]
        rstd_ready = [None] + [sem(f"rstd_ready{n}") for n in (1, 2, 3)]
        shift_ready = [None] + [sem(f"shift_ready{n}") for n in (1, 2, 3)]
        z_ready = [None] + [sem(f"z_ready{n}") for n in (1, 2, 3)]
        turned_ready = [None] + [sem(f"turned_ready{n}") for n in (1, 2, 3)]
        minus_mean_ready = [None] + [sem(f"minus_mean_ready{n}") for n in (1, 2, 3)]
        square_sum_ready = [None, None] + [sem(f"square_sum_ready{n}") for n in (2, 3)]
        high_ready = [None, sem("high_ready1"), None, sem("high_ready3")]
        low_ready = [None, sem("low_ready1"), None, sem("low_ready3")]
        product_ready = [None, sem("ffn1_ready"), sem("wo_ready"), sem("ffn3_ready")]
        x_ready = [None] + [sem(f"x{n}_ready") for n in (1, 2, 3)]
        scaled_ready = sem("scaled_ready")
        mixed_ready = sem("mixed_ready")
        k_ready, v_ready, r_ready = sem("k_ready"), sem("v_ready"), sem("r_ready")
        exp_k_ready = sem("exp_k_ready")
        tanh_ready = sem("tanh_ready")
        kv_ready = sem("kv_ready")
        clamped_ready = sem("clamped_ready")
        k_state_ready = sem("k_state_ready")
        v_state_ready = sem("v_state_ready")
        first_k_ready = sem("first_k_ready")
        wk_ready = sem("wk_ready")
        wv_ready = sem("wv_ready")
        gated_ready = sem("gated_ready")
        guess_ready = sem("guess_ready")
        s_ready = sem("s_ready")
        guessed_ready = sem("guessed_ready")
        square_ready = sem("square_ready")
        linear_ready = sem("linear_ready")
        rwkv_ready = sem("rwkv_ready")

        def run_steps(engine, last_lag, step):
            loop_from = 4
            loop_to = SEQS - (SEQS - loop_from) % 2
            for t in range(loop_from):
                step(t, t % 2, lambda lag: 0 <= t - lag < SEQS)
            with engine.Fori(loop_from, loop_to - 1, 2) as t:
                step(t, 0, lambda lag: True)
                step(t + 1, 1, lambda lag: True)
            for t in range(loop_to, SEQS + last_lag):
                step(t, t % 2, lambda lag: 0 <= t - lag < SEQS)

        def beyond(b, n):
            return not isinstance(b, int) or b >= n

        norm_first, norm_last = (0,), (SEQS - 1,)
        by_vector_before = [None, len(norm_first), len(norm_first), 0]

        def by_vector(n, b):
            return isinstance(b, int) and b in (norm_first if n < 3 else norm_last)

        block = ctx.enter_context(nc.Block())

        @block.sync
        def _(sp):
            def load(b, p):
                if beyond(b, 2):
                    sp.wait_ge(x_ready[1], TT * (b - 1))
                sp.dma_start(X0[:, p], x_dram[bass.ds(b, 1)].rearrange("s p j c -> p (s j) c")
                             if not isinstance(b, int) else x_dram[b]).then_inc(x_loaded[p], 16)

            def hold(b, p):
                sp.wait_ge(x_ready[1], TT * (b + 1))
                if beyond(b, 2):
                    sp.wait_ge(x_ready[2], TT * (b - 1))
                sp.dma_start(X1_held[:, p], X1[:, p]).then_inc(x1_held[p], 16)

            def store(b, p):
                if isinstance(b, int) and b == SEQS - 1:
                    for h in range(2):
                        half = slice(2 * h, 2 * h + 2)
                        sp.wait_ge(x_ready[3], TT * b + 2 * (h + 1))
                        sp.dma_start(out_dram[b][:, half], X3[:, p, half]).then_inc(out_stored[p], 16)
                    return
                sp.wait_ge(x_ready[3], TT * (b + 1))
                sp.dma_start(out_dram[bass.ds(b, 1)].rearrange("s p j c -> p (s j) c")
                             if not isinstance(b, int) else out_dram[b], X3[:, p]).then_inc(out_stored[p], 16)

            sp.dma_start(X0[:, 0, 0:TT // 2], x_dram[0][:, 0:TT // 2]).then_inc(first_half_loaded, 16)
            sp.dma_start(X0[:, 0, TT // 2:TT], x_dram[0][:, TT // 2:TT]).then_inc(x_loaded[0], 16)
            sp.dma_start(w_f[:, :, :], ffn_t.rearrange("(k p) o -> p k o", p=P)).then_inc(ffn_loaded, 16)
            for vec, dram in ((decay_in, time_decay), (first_in, time_first), (mix, time_mix)):
                sp.dma_start(vec[:, :], dram).then_inc(vectors_loaded, 16)
            for w, dram in ((w_k, wk_t), (w_v, wv_t), (w_r, wr_t), (w_o, wo_t)):
                sp.dma_start(w[:, :, :], dram.rearrange("(k p) o -> p k o", p=P)).then_inc(weights_loaded, 16)
            load(1, 1)

            def step(t, u, has):
                if has(0) and beyond(t, 2):
                    load(t, u)
                if has(1):
                    hold(t - 1, 1 - u)
                if has(4):
                    store(t - 4, u)

            run_steps(sp, 4, step)
            for parity, stored in enumerate(out_stored):
                sp.wait_ge(stored, 8 * SEQS + 1 + (16 if parity == (SEQS - 1) % 2 else 0))

        @block.gpsimd
        def _(pool):
            nc.gpsimd.memset(ident[:, :], 0.0).then_inc(gpsimd_consts, 1)
            nc.gpsimd.memset(half_power[:, :], -0.5).then_inc(gpsimd_consts, 1)
            nc.gpsimd.memset(warm[:, :], 1.0).then_inc(warm_filled, 1)
            pool.wait_ge(gpsimd_consts, 2)
            nc.gpsimd.affine_select(out=ident[:, :], in_=ident[:, :], compare_op=ALU.not_equal, fill=1.0,
                                    base=0, pattern=[[-1, P]], channel_multiplier=1).then_inc(gpsimd_consts, 1)

            def inverse_std(n, b, p):
                pool.wait_ge(var_ready[n], b + 1)
                if beyond(b, 1):
                    pool.wait_ge(z_ready[n], TT * b)
                nc.gpsimd.tensor_tensor(rstd[n][:, :], var_eps[n][:, :], half_power[:, :],
                                        ALU.pow).then_inc(rstd_ready[n], 1)

            def normalize_1(b, p):
                if by_vector(1, b):
                    return
                pool.wait_ge(rstd_ready[1], b + 1)
                pool.wait_ge(minus_mean_ready[1], b + 1 - by_vector_before[1])
                if beyond(b, 1):
                    pool.wait_ge(z_ready[1], TT * b)
                nc.gpsimd.tensor_tensor(shift[1][:, :], minus_mean[1][:, :], rstd[1][:, :],
                                        ALU.mult).then_inc(shift_ready[1], 1)
                pool.wait_ge(shift_ready[1], b + 1 - by_vector_before[1])
                if beyond(b, 1):
                    pool.wait_ge(turned_ready[1], b)
                pool.nop(nofuse=True)
                for j in range(TT):
                    nc.gpsimd.tensor_scalar(Z[1][:, j], X0[:, p, j], rstd[1][:, j:j + 1], shift[1][:, j:j + 1],
                                            ALU.mult, ALU.add).then_inc(z_ready[1], 1)

            def denominator(b, p, m):
                pool.wait_ge(first_k_ready, CH * b + m + 1)
                pool.wait_ge(k_state_ready, CH * b + m + 1)
                if beyond(b, 2):
                    pool.wait_ge(guess_ready, CH * (b - 1))
                nc.gpsimd.tensor_tensor(WK[:, p, m], FK[:, p, m], SK[:, p, m, 0:T], ALU.add).then_inc(wk_ready, 1)

            def times_guess(b, p, m):
                pool.wait_ge(guess_ready, CH * b + m + 1)
                if beyond(b, 2):
                    pool.wait_ge(linear_ready, CH * (b - 1))
                    pool.wait_ge(square_ready, CH * (b - 1))
                nc.gpsimd.tensor_tensor(SS[:, p, m], WK[:, p, m], Y0[:, p, m], ALU.mult).then_inc(s_ready, 1)

            def numerator_times_guess(b, p, m):
                pool.wait_ge(gated_ready, CH * b + m + 1)
                pool.wait_ge(guess_ready, CH * b + m + 1)
                nc.gpsimd.tensor_tensor(WV[:, p, m], WV[:, p, m], Y0[:, p, m],
                                        ALU.mult).then_inc(guessed_ready, 1)

            def step(t, u, has):
                if has(0):
                    inverse_std(1, t, u)
                    normalize_1(t, u)
                if has(2):
                    times_guess(t - 2, u, 1)
                if has(3):
                    inverse_std(3, t - 3, 1 - u)
                if has(2):
                    numerator_times_guess(t - 2, u, 1)
                if has(1):
                    denominator(t - 1, 1 - u, 0)
                if has(0):
                    inverse_std(2, t, u)
                if has(1):
                    times_guess(t - 1, 1 - u, 0)
                    denominator(t - 1, 1 - u, 1)
                    numerator_times_guess(t - 1, 1 - u, 0)

            run_steps(pool, 3, step)

        @block.scalar
        def _(act):
            act.wait_ge(vectors_loaded, 48)
            nc.scalar.activation(decay_exp[:, :], decay_in[:, :], ACT.Exp).then_inc(act_vectors, 1)
            nc.scalar.activation(first_w[:, :], first_in[:, :], ACT.Exp).then_inc(act_vectors, 1)
            act.wait_ge(act_vectors, 2)
            nc.scalar.activation(decay[:, :], decay_exp[:, :], ACT.Exp, scale=-1.0).then_inc(act_decay, 1)
            act.wait_ge(ffn_loaded, 16)
            nc.scalar.activation(w_abs[:, :, :], w_f[:, :, :], ACT.Abs,
                                 accum_out=abs_sum[:, :]).then_inc(abs_summed, 1)

            def normalize(n, b, p):
                if by_vector(n, b):
                    return
                act.wait_ge(shift_ready[n], b + 1 - by_vector_before[n])
                if beyond(b, 1):
                    act.wait_ge(turned_ready[n], b)
                for j in range(TT):
                    nc.scalar.activation(Z[n][:, j], XS[n - 1][:, p, j], ACT.Identity, bias=shift[n][:, j:j + 1],
                                         scale=rstd[n][:, j:j + 1]).then_inc(z_ready[n], 1)

            def sum_squares(n, b, p, j):
                if by_vector(n, b):
                    return
                act.wait_ge(minus_mean_ready[n], b + 1 - by_vector_before[n])
                if beyond(b, 1):
                    act.wait_ge(var_ready[n], b)
                nc.scalar.activation(squares[:, j], XS[n - 1][:, p, j], ACT.Square, bias=minus_mean[n][:, j:j + 1],
                                     accum_out=square_sum[n][:, j:j + 1]).then_inc(square_sum_ready[n], 1)

            def high_half(n, b, p, m):
                act.wait_ge(turned_ready[n], b + 1)
                if beyond(b, 1):
                    act.wait_ge(product_ready[n], 2 * b)
                nc.scalar.activation(z_high[n][:, m], turned[m][:, :], ACT.Copy).then_inc(high_ready[n], 1)

            def scale_mix(b, p, m):
                act.wait_ge(turned_ready[2], b + 1)
                if beyond(b, 2):
                    act.wait_ge(r_ready, CH * (b - 1))
                nc.scalar.activation(XM[:, p, m], turned[m][:, :], ACT.Identity,
                                     scale=mix[:, m:m + 1]).then_inc(scaled_ready, 1)

            def clamp_k(b, p, m):
                act.wait_ge(k_ready, CH * b + m + 1)
                k = ring_bank(p, "k", m)[:, :]
                nc.scalar.activation(k, k, ACT.Relu, scale=-1.0, bias=K_CLAMP).then_inc(clamped_ready, 1)

            def exp_k(b, p, m):
                act.wait_ge(clamped_ready, CH * b + m + 1)
                if beyond(b, 2):
                    act.wait_ge(k_state_ready, CH * (b - 1))
                    act.wait_ge(kv_ready, CH * (b - 1))
                nc.scalar.activation(EK[:, p, m], ring_bank(p, "k", m)[:, :], ACT.Exp, scale=-1.0,
                                     bias=K_CLAMP).then_inc(exp_k_ready, 1)

            def first_k(b, p, m):
                act.wait_ge(exp_k_ready, CH * b + m + 1)
                if beyond(b, 2):
                    act.wait_ge(wk_ready, CH * (b - 1))
                nc.scalar.activation(FK[:, p, m], EK[:, p, m], ACT.Identity, scale=first_w[:, m:m + 1],
                                     bias=WKV_EPS).then_inc(first_k_ready, 1)

            def tanh_r(b, p, m):
                act.wait_ge(r_ready, CH * b + m + 1)
                if beyond(b, 2):
                    act.wait_ge(gated_ready, CH * (b - 1))
                nc.scalar.activation(TH[:, p, m], ring_bank(p, "r", m)[:, :], ACT.Tanh,
                                     scale=-0.5).then_inc(tanh_ready, 1)

            def guess(b, p, m):
                act.wait_ge(wk_ready, CH * b + m + 1)
                if beyond(b, 2):
                    act.wait_ge(s_ready, CH * (b - 1))
                    act.wait_ge(guessed_ready, CH * (b - 1))
                nc.scalar.activation(Y0[:, p, m], WK[:, p, m].bitcast(i32), ACT.Exp, scale=RC["guess_scale"],
                                     bias=RC["guess_bias"]).then_inc(guess_ready, 1)

            def square(b, p, m):
                act.wait_ge(s_ready, CH * b + m + 1)
                if beyond(b, 2):
                    act.wait_ge(rwkv_ready, CH * (b - 1))
                nc.scalar.activation(QQ[:, p, m], SS[:, p, m], ACT.Square,
                                     scale=RC["square_scale"], bias=RC["square_bias"]).then_inc(square_ready, 1)

            def step(t, u, has):
                if has(2):
                    guess(t - 2, u, 0)
                    first_k(t - 2, u, 1)
                if has(1):
                    normalize(2, t - 1, 1 - u)
                if has(2):
                    guess(t - 2, u, 1)
                if has(1):
                    scale_mix(t - 1, 1 - u, 0)
                    scale_mix(t - 1, 1 - u, 1)
                if has(2):
                    square(t - 2, u, 0)
                if has(3):
                    for j in range(TT):
                        sum_squares(3, t - 3, 1 - u, j)
                if has(2):
                    tanh_r(t - 2, u, 1)
                if has(1):
                    clamp_k(t - 1, 1 - u, 0)
                if has(0):
                    high_half(1, t, u, 0)
                    high_half(1, t, u, 1)
                if has(1):
                    exp_k(t - 1, 1 - u, 0)
                if has(2):
                    square(t - 2, u, 1)
                if has(3):
                    normalize(3, t - 3, 1 - u)
                if has(1):
                    first_k(t - 1, 1 - u, 0)
                    tanh_r(t - 1, 1 - u, 0)
                if has(3):
                    high_half(3, t - 3, 1 - u, 0)
                    high_half(3, t - 3, 1 - u, 1)
                if has(0):
                    sum_squares(2, t, u, 0)
                    sum_squares(2, t, u, 1)
                if has(1):
                    clamp_k(t - 1, 1 - u, 1)
                if has(0):
                    sum_squares(2, t, u, 2)
                    sum_squares(2, t, u, 3)
                if has(1):
                    exp_k(t - 1, 1 - u, 1)

            run_steps(act, 3, step)

        @block.vector
        def _(dve):
            nc.vector.memset(ones[:, :], 1.0).then_inc(dve_ones, 1)
            nc.vector.memset(decay_rows[:, :, :], 1.0).then_inc(dve_consts, 1)
            for parity, stored in enumerate(out_stored):
                nc.vector.memset(X3[:, parity, 0, 0:1], 0.0).then_inc(stored, 1)
            for state in (SK, SV):
                nc.vector.memset(state[:, :, :, 0:1], 0.0).then_inc(dve_consts, 1)

            def spread_decay():
                dve.wait_ge(act_decay, 1)
                dve.wait_ge(dve_consts, 3)
                for m in range(CH):
                    nc.vector.tensor_scalar(decay_rows[:, m], decay_rows[:, m], decay[:, m:m + 1], None,
                                            ALU.mult).then_inc(dve_consts, 1)
                nc.vector.tensor_scalar(mix_rest[:, :], mix[:, :], -1.0, 1.0, ALU.mult,
                                        ALU.add).then_inc(dve_consts, 1)

            def quantize():
                dve.wait_ge(scale_summed, 1)
                nc.vector.tensor_scalar(half_scale[:, :], tokens[0][:, 0:1], 0.5 / (C * C), 0.5 * QUANT_EPS, ALU.mult,
                                        ALU.max).then_inc(scale_ready, 1)
                dve.wait_ge(scale_ready, 1)
                nc.vector.tensor_scalar(minus_half_scale[:, :], half_scale[:, :], -1.0, None,
                                        ALU.mult).then_inc(scale_ready, 1)
                dve.wait_ge(scale_ready, 2)
                nc.vector.tensor_scalar(w_below[:, :, :], w_f[:, :, :], minus_half_scale[:, :], None,
                                        ALU.is_lt).then_inc(below_ready, 1)
                dve.wait_ge(below_ready, 1)
                nc.vector.scalar_tensor_tensor(ternary[:, :, :], w_f[:, :, :], half_scale[:, :], w_below[:, :, :],
                                               ALU.is_gt, ALU.subtract).then_inc(ternary_ready, 1)

            def stats(n, b, p, j):
                if n == 1:
                    if isinstance(b, int) and b == 0 and j < TT // 2:
                        dve.wait_ge(first_half_loaded, 16)
                    else:
                        dve.wait_ge(x_loaded[p], 8 * (b - p) + 16)
                else:
                    dve.wait_ge(x_ready[n - 1], TT * b + j + 1)
                nc.vector.bn_stats(bn[n][:, j], XS[n - 1][:, p, j]).then_inc(stats_ready[n], 1)

            def variance(n, b, p):
                count = TT * (b + 1) if n < 3 else TT * (b + 1 - SEQS + len(norm_last))
                dve.wait_ge(stats_ready[n], count)
                if beyond(b, 1):
                    dve.wait_ge(z_ready[n], TT * b)
                dve.nop(nofuse=True)
                for j in range(TT):
                    nc.vector.bn_aggr(mean_var[n][:, j], bn[n][:, j]).then_inc(mean_ready[n], 1)
                dve.wait_ge(mean_ready[n], count)
                if beyond(b, 1):
                    dve.wait_ge(rstd_ready[n], b)
                nc.vector.tensor_scalar(var_eps[n][:, :], mean_var[n][:, :, 1], LN_EPS, None,
                                        ALU.add).then_inc(var_ready[n], 1)
                if n == 1 and not by_vector(1, b):
                    nc.vector.tensor_scalar(minus_mean[1][:, :], mean_var[1][:, :, 0], -1.0, None,
                                            ALU.mult).then_inc(minus_mean_ready[1], 1)
                if n == 1 and by_vector(1, b):
                    normalize_here(1, b, p)
                    if b == 0:
                        quantize()

            def normalize_here(n, b, p):
                dve.wait_ge(rstd_ready[n], b + 1)
                if b:
                    dve.wait_ge(turned_ready[n], b)
                for j in range(TT):
                    nc.vector.tensor_scalar(Z[n][:, j], XS[n - 1][:, p, j], mean_var[n][:, j, 0:1],
                                            rstd[n][:, j:j + 1], ALU.subtract, ALU.mult).then_inc(z_ready[n], 1)

            def negate_mean(n, b, p):
                if by_vector(n, b):
                    return
                dve.wait_ge(x_ready[n - 1], TT * (b + 1))
                if beyond(b, 1 + by_vector_before[n]):
                    dve.wait_ge(square_sum_ready[n], TT * (b - by_vector_before[n]))
                    dve.wait_ge(shift_ready[n], b - by_vector_before[n])
                nc.vector.tensor_scalar(minus_mean[n][:, :], row_sum[n][:, :], -1.0 / C, None,
                                        ALU.mult).then_inc(minus_mean_ready[n], 1)

            def variance_of_squares(n, b, p):
                if by_vector(n, b):
                    return
                dve.wait_ge(square_sum_ready[n], TT * (b + 1 - by_vector_before[n]))
                if beyond(b, 1):
                    dve.wait_ge(rstd_ready[n], b)
                nc.vector.tensor_scalar(var_eps[n][:, :], square_sum[n][:, :], 1.0 / C, LN_EPS, ALU.mult,
                                        ALU.add).then_inc(var_ready[n], 1)

            def shifts(n, b, p):
                if by_vector(n, b):
                    return
                dve.wait_ge(rstd_ready[n], b + 1)
                if beyond(b, 1):
                    dve.wait_ge(z_ready[n], TT * b)
                nc.vector.tensor_tensor(shift[n][:, :], minus_mean[n][:, :], rstd[n][:, :],
                                        ALU.mult).then_inc(shift_ready[n], 1)

            def low_half(n, b, p, m):
                dve.wait_ge(high_ready[n], CH * b + m + 1)
                if beyond(b, 1):
                    dve.wait_ge(product_ready[n], 2 * b)
                nc.vector.tensor_tensor(z_low[n][:, m], turned[m][:, :], z_high[n][:, m],
                                        ALU.subtract).then_inc(low_ready[n], 1)

            def residual(n, b, p, h):
                if n == 1 and h == 0 and isinstance(b, int) and b == 0:
                    spread_decay()
                dve.wait_ge(product_ready[n], 2 * b + h + 1)
                if n == 1:
                    dve.wait_ge(z_ready[1], TT * (b + 1))
                if n == 3 and beyond(b, 2):
                    dve.wait_ge(out_stored[p], 8 * (b - p) + 1)
                if n == 1 and beyond(b, 2):
                    dve.wait_ge(z_ready[2], TT * (b - 1))
                    dve.wait_ge(x1_held[p], 8 * (b - p))
                if n == 2:
                    dve.wait_ge(x1_held[p], 8 * (b - p) + 16)
                    if beyond(b, 2):
                        dve.wait_ge(z_ready[3], TT * (b - 1))
                        dve.wait_ge(x_ready[3], TT * (b - 1))
                if n < 3 and beyond(b, 1 + by_vector_before[n + 1]):
                    dve.wait_ge(minus_mean_ready[n + 1], b - by_vector_before[n + 1])
                old = (X1_held if n == 2 else XS[n - 1])[:, p]
                bank = tokens[h][:, :].rearrange("p (j c) -> p j c", c=C)
                if n == 3:
                    half = slice(2 * h, 2 * h + 2)
                    nc.vector.scalar_tensor_tensor(X3[:, p, half], bank, half_scale[:, :], old[:, half], ALU.mult,
                                                   ALU.add).then_inc(x_ready[3], 2)
                    return
                for j in (2 * h, 2 * h + 1):
                    factor = half_scale[:, :] if n == 1 else 1.0
                    nc.vector.scalar_tensor_tensor(XS[n][:, p, j], bank[:, j % 2], factor, old[:, j], ALU.mult, ALU.add,
                                                   accum_out=row_sum[n + 1][:, j:j + 1]).then_inc(x_ready[n], 1)
                if by_vector(n + 1, b):
                    for j in (2 * h, 2 * h + 1):
                        stats(n + 1, b, p, j)
                    if h == 1:
                        variance(n + 1, b, p)
                        normalize_here(n + 1, b, p)

            def token_mix(b, p, m):
                if m == 0 and isinstance(b, int) and b == 0:
                    dve.wait_ge(dve_consts, DVE_CONSTS)
                dve.wait_ge(scaled_ready, CH * b + m + 1)
                nc.vector.scalar_tensor_tensor(XM[:, p, m, 1:T], turned[m][:, 0:T - 1], mix_rest[:, m:m + 1],
                                               XM[:, p, m, 1:T], ALU.mult, ALU.add).then_inc(mixed_ready, 1)

            def key_value(b, p, m):
                dve.wait_ge(exp_k_ready, CH * b + m + 1)
                dve.wait_ge(v_ready, CH * b + m + 1)
                nc.vector.tensor_tensor(KV[:, p, m], EK[:, p, m], ring_bank(p, "v", m)[:, :],
                                        ALU.mult).then_inc(kv_ready, 1)

            def k_state(b, p, m):
                dve.wait_ge(exp_k_ready, CH * b + m + 1)
                if beyond(b, 2):
                    dve.wait_ge(wk_ready, CH * (b - 1))
                nc.vector.tensor_tensor_scan(SK[:, p, m, 1:T + 1], decay_rows[:, m], EK[:, p, m], 0.0, ALU.mult,
                                             ALU.add).then_inc(k_state_ready, 1)

            def v_state(b, p, m):
                dve.wait_ge(kv_ready, CH * b + m + 1)
                nc.vector.tensor_tensor_scan(SV[:, p, m, 1:T + 1], decay_rows[:, m], KV[:, p, m], 0.0, ALU.mult,
                                             ALU.add).then_inc(v_state_ready, 1)

            def numerator(b, p, m):
                dve.wait_ge(v_state_ready, CH * b + m + 1)
                nc.vector.scalar_tensor_tensor(WV[:, p, m], KV[:, p, m], first_w[:, m:m + 1], SV[:, p, m, 0:T],
                                               ALU.mult, ALU.add).then_inc(wv_ready, 1)

            def gate(b, p, m):
                dve.wait_ge(tanh_ready, CH * b + m + 1)
                dve.wait_ge(wv_ready, CH * b + m + 1)
                nc.vector.scalar_tensor_tensor(WV[:, p, m], TH[:, p, m], -1.0, WV[:, p, m], ALU.add,
                                               ALU.mult).then_inc(gated_ready, 1)

            def linear(b, p, m):
                dve.wait_ge(guessed_ready, CH * b + m + 1)
                dve.wait_ge(s_ready, CH * b + m + 1)
                nc.vector.scalar_tensor_tensor(WV[:, p, m], SS[:, p, m], -RC["root"], WV[:, p, m], ALU.add,
                                               ALU.mult).then_inc(linear_ready, 1)

            def rwkv(b, p, m):
                dve.wait_ge(square_ready, CH * b + m + 1)
                dve.wait_ge(linear_ready, CH * b + m + 1)
                if beyond(b, 2):
                    dve.wait_ge(product_ready[2], 2 * (b - 1))
                nc.vector.scalar_tensor_tensor(F[:, p, m], QQ[:, p, m], RC["rest"], WV[:, p, m], ALU.add,
                                               ALU.mult).then_inc(rwkv_ready, 1)

            def step(t, u, has):
                if has(0):
                    for j in range(TT):
                        stats(1, t, u, j)
                    variance(1, t, u)
                if has(2):
                    key_value(t - 2, u, 1)
                if has(1):
                    token_mix(t - 1, 1 - u, 0)
                    token_mix(t - 1, 1 - u, 1)
                if has(2):
                    v_state(t - 2, u, 1)
                    linear(t - 2, u, 0)
                    numerator(t - 2, u, 1)
                if has(3):
                    variance_of_squares(3, t - 3, 1 - u)
                if has(2):
                    rwkv(t - 2, u, 0)
                    gate(t - 2, u, 1)
                if has(0):
                    low_half(1, t, u, 0)
                if has(3):
                    shifts(3, t - 3, 1 - u)
                if has(0):
                    low_half(1, t, u, 1)
                if has(1):
                    key_value(t - 1, 1 - u, 0)
                    k_state(t - 1, 1 - u, 0)
                if has(2):
                    linear(t - 2, u, 1)
                if has(1):
                    v_state(t - 1, 1 - u, 0)
                if has(0):
                    residual(1, t, u, 0)
                    residual(1, t, u, 1)
                    negate_mean(2, t, u)
                if has(2):
                    rwkv(t - 2, u, 1)
                if has(1):
                    numerator(t - 1, 1 - u, 0)
                if has(3):
                    low_half(3, t - 3, 1 - u, 0)
                if has(1):
                    gate(t - 1, 1 - u, 0)
                if has(3):
                    low_half(3, t - 3, 1 - u, 1)
                if has(0):
                    variance_of_squares(2, t, u)
                if has(2):
                    residual(2, t - 2, u, 0)
                if has(1):
                    k_state(t - 1, 1 - u, 1)
                if has(0):
                    shifts(2, t, u)
                if has(2):
                    residual(2, t - 2, u, 1)
                if has(3):
                    residual(3, t - 3, 1 - u, 0)
                if has(2):
                    negate_mean(3, t - 2, u)
                if has(3):
                    residual(3, t - 3, 1 - u, 1)

            run_steps(dve, 3, step)

        @block.tensor
        def _(pe):
            def warm_up(count, bank):
                for _ in range(count):
                    nc.tensor.matmul(bank[:, :], warm[:, 0:P], warm[:, :], start=True, stop=True)

            pe.wait_ge(warm_filled, 1)
            warm_up(WARM_START, ring[3])
            pe.wait_ge(dve_ones, 1)
            pe.wait_ge(abs_summed, 1)
            nc.tensor.matmul(tokens[0][:, 0:1], ones[:, :], abs_sum[:, :], start=True,
                             stop=True).then_inc(scale_summed, 1)
            pe.wait_ge(gpsimd_consts, 3)

            def bank_free(readers, per_batch, b, upto):
                if isinstance(b, int):
                    if b < 0:
                        return
                    b = min(b, SEQS - 1)
                pe.wait_ge(readers, per_batch * b + upto)

            def turn(n, b, p, after):
                if n == 2 and isinstance(b, int) and b == 0:
                    warm_up(WARM_TURN, ring[3])
                if n == 3 and isinstance(b, int) and b == SEQS - 2:
                    pe.wait_ge(last_reader[RING[2][0]], CH * (SEQS - 1) + RING[2][1] + 1)
                    warm_up(WARM_LAST_TURN, ring[0])
                for m, last_b in after.items():
                    bank_free(mixed_ready if m == 2 else low_ready[m], CH, last_b, CH)
                for j in range(TT):
                    pe.wait_ge(z_ready[n], TT * b + j + 1)
                    for m in range(CH):
                        last = nc.tensor.transpose(turned[m][:, j * P:(j + 1) * P], Z[n][:, j, m * P:(m + 1) * P],
                                                   ident[:, :])
                last.then_inc(turned_ready[n], 1)

            def ffn(n, b, p, h, after):
                for m, last_b in after.items():
                    bank_free(x_ready[m], TT, last_b, 2 * (h + 1))
                if n == 1 and isinstance(b, int) and b == 0:
                    pe.wait_ge(ternary_ready, 1)
                if n == 3 and h == 0 and isinstance(b, int) and b >= SEQS - 2:
                    warm_up(WARM_LAST_FFN, ring[0])
                pe.wait_ge(low_ready[n], CH * (b + 1))
                for j in (2 * h, 2 * h + 1):
                    o = tokens[h][:, (j % 2) * C:(j % 2 + 1) * C]
                    parts = [(part, m) for m in range(CH) for part in (z_high[n], z_low[n])]
                    for i, (part, m) in enumerate(parts):
                        last = nc.tensor.matmul(o, part[:, m, j * P:(j + 1) * P], ternary[:, m],
                                                start=i == 0, stop=i == len(parts) - 1)
                last.then_inc(product_ready[n], 1)

            def output_product(b, p, h, after):
                for m, last_b in after.items():
                    bank_free(x_ready[m], TT, last_b, 2 * (h + 1))
                pe.wait_ge(rwkv_ready, CH * (b + 1))
                for j in (2 * h, 2 * h + 1):
                    o = tokens[h][:, (j % 2) * C:(j % 2 + 1) * C]
                    for m in range(CH):
                        last = nc.tensor.matmul(o, F[:, p, m, j * P:(j + 1) * P], w_o[:, m],
                                                start=m == 0, stop=m == CH - 1)
                last.then_inc(product_ready[2], 1)

            last_reader = {"k": exp_k_ready, "v": kv_ready, "r": tanh_ready}

            def project(b, p, kind, m):
                use = RING.index((kind, m))
                kind_before, m_before = RING[use - 4]
                if isinstance(b, int) and b == 0 and use == 0:
                    warm_up(WARM_PROJECT, ring[3])
                if use >= 4 or beyond(b, 1):
                    pe.wait_ge(last_reader[kind_before], CH * (b if use >= 4 else b - 1) + m_before + 1)
                pe.wait_ge(mixed_ready, CH * (b + 1))
                if isinstance(b, int) and b == 0:
                    pe.wait_ge(weights_loaded, 64)
                w, ready = {"k": (w_k, k_ready), "v": (w_v, v_ready), "r": (w_r, r_ready)}[kind]
                for c in range(CH):
                    last = nc.tensor.matmul(ring_bank(p, kind, m)[:, :], w[:, c, m * P:(m + 1) * P], XM[:, p, c],
                                            start=c == 0, stop=c == CH - 1)
                last.then_inc(ready, 1)

            def step(t, u, has):
                if has(0):
                    turn(1, t, u, after={1: t - 1, 2: t - 1, 3: t - 4})
                if has(1):
                    project(t - 1, 1 - u, "v", 0)
                    project(t - 1, 1 - u, "r", 0)
                if has(0):
                    ffn(1, t, u, 0, after={1: t - 1, 2: t - 3, 3: t - 4})
                    ffn(1, t, u, 1, after={1: t - 1, 2: t - 3, 3: t - 4})
                if has(3):
                    turn(3, t - 3, 1 - u, after={1: t, 2: t - 1, 3: t - 4})
                if has(1):
                    project(t - 1, 1 - u, "k", 1)
                if has(2):
                    output_product(t - 2, u, 0, after={1: t, 2: t - 3, 3: t - 4})
                    output_product(t - 2, u, 1, after={1: t, 2: t - 3, 3: t - 4})
                if has(3):
                    ffn(3, t - 3, 1 - u, 0, after={1: t, 2: t - 2, 3: t - 4})
                    ffn(3, t - 3, 1 - u, 1, after={1: t, 2: t - 2, 3: t - 4})
                if has(1):
                    project(t - 1, 1 - u, "v", 1)
                if has(0):
                    turn(2, t, u, after={1: t, 2: t - 1, 3: t - 3})
                if has(1):
                    project(t - 1, 1 - u, "r", 1)
                if has(0):
                    project(t, u, "k", 0)

            run_steps(pe, 3, step)


_OUT = "out"


def kernel(L0_attn_x, L0_attn_time_decay, L0_attn_time_first, L0_attn_time_mix, L0_attn_Wk, L0_attn_Wv, L0_attn_Wr,
           L0_attn_Wo, L0_ffn_weight):
    import concourse.bacc as bacc
    from concourse.bass_utils import run_bass_kernel_spmd

    def turned(w):
        return np.ascontiguousarray(np.asarray(w).T)

    def by_partition(v):
        return np.ascontiguousarray(np.asarray(v).reshape(-1, P).T)

    arrays = {
        "x": np.ascontiguousarray(L0_attn_x),
        "time_decay": by_partition(L0_attn_time_decay),
        "time_first": by_partition(L0_attn_time_first),
        "time_mix": by_partition(L0_attn_time_mix),
        "wk_t": turned(L0_attn_Wk),
        "wv_t": turned(L0_attn_Wv),
        "wr_t": turned(L0_attn_Wr),
        "wo_t": turned(L0_attn_Wo),
        "ffn_t": turned(L0_ffn_weight),
    }
    nc = bacc.Bacc("TRN2", target_bir_lowering=False, num_devices=1)
    args = [nc.dram_tensor(name, a.shape, mybir.dt.from_np(a.dtype), kind="ExternalInput").ap()
            for name, a in arrays.items()]
    x_shape = arrays["x"].shape
    out = nc.dram_tensor(_OUT, x_shape, mybir.dt.float32, kind="ExternalOutput").ap()
    macaron(nc, *args, out)
    result = run_bass_kernel_spmd(nc, [arrays], core_ids=[0])
    return result.results[0][_OUT]
```
